# Optimizing a Trainium2 kernel written in Bass

```python
import numpy as np
import jax
import jax.numpy as jnp

def _softmax(x, axis=-1):
    return jax.nn.softmax(x, axis=axis)

def _gelu(x):
    return jax.nn.gelu(x, approximate=True)

def _silu(x):
    return jax.nn.silu(x)

def _sigmoid(x):
    return jax.nn.sigmoid(x)

def _layernorm(x, axis=-1, eps=1e-05):
    m = jnp.mean(x, axis=axis, keepdims=True)
    v = jnp.var(x, axis=axis, keepdims=True)
    return (x - m) / jnp.sqrt(v + eps)

def _scatter_add(tgt, idx, src, axis=0):
    return tgt.at[idx].add(src)

def _segment_sum(src, seg, n):
    return jax.ops.segment_sum(src, seg, n)
kernel_name = 'mk_dlrm_tower_d1_rec_r8_c9d72b'

def setup_inputs(seed: int=0):
    np.random.seed(seed)
    _w = jnp.asarray

    def _rec_inputs():
        import jax
        import jax.numpy as jnp
        _tk = jax.random.key(seed)
        dense_ctx = jax.random.normal(jax.random.fold_in(_tk, 190), (1024, 16), jnp.float32)
        ids = jnp.stack([jax.random.randint(jax.random.fold_in(_tk, 200 + f), (1024,), 0, v, jnp.int32) for f, v in enumerate([1000, 1000, 1250, 125000, 12500, 1000, 12500, 1250, 1000, 1250, 1250, 1000, 1000, 125000, 1000, 1250, 125000, 1000, 1250, 125000, 1000, 12500, 1000, 1250, 1250, 12500, 1250, 125000, 125000, 125000, 12500, 1250, 125000, 125000, 1000, 1000, 125000, 1250, 12500])], axis=1)
        tbl_0 = 0.05 * jax.random.normal(jax.random.fold_in(_tk, 500 + 0), (1000, 16), jnp.float32)
        tbl_1 = 0.05 * jax.random.normal(jax.random.fold_in(_tk, 500 + 1), (1000, 16), jnp.float32)
        tbl_2 = 0.05 * jax.random.normal(jax.random.fold_in(_tk, 500 + 2), (1250, 16), jnp.float32)
        tbl_3 = 0.05 * jax.random.normal(jax.random.fold_in(_tk, 500 + 3), (125000, 16), jnp.float32)
        tbl_4 = 0.05 * jax.random.normal(jax.random.fold_in(_tk, 500 + 4), (12500, 16), jnp.float32)
        tbl_5 = 0.05 * jax.random.normal(jax.random.fold_in(_tk, 500 + 5), (1000, 16), jnp.float32)
        tbl_6 = 0.05 * jax.random.normal(jax.random.fold_in(_tk, 500 + 6), (12500, 16), jnp.float32)
        tbl_7 = 0.05 * jax.random.normal(jax.random.fold_in(_tk, 500 + 7), (1250, 16), jnp.float32)
        tbl_8 = 0.05 * jax.random.normal(jax.random.fold_in(_tk, 500 + 8), (1000, 16), jnp.float32)
        tbl_9 = 0.05 * jax.random.normal(jax.random.fold_in(_tk, 500 + 9), (1250, 16), jnp.float32)
        tbl_10 = 0.05 * jax.random.normal(jax.random.fold_in(_tk, 500 + 10), (1250, 16), jnp.float32)
        tbl_11 = 0.05 * jax.random.normal(jax.random.fold_in(_tk, 500 + 11), (1000, 16), jnp.float32)
        tbl_12 = 0.05 * jax.random.normal(jax.random.fold_in(_tk, 500 + 12), (1000, 16), jnp.float32)
        tbl_13 = 0.05 * jax.random.normal(jax.random.fold_in(_tk, 500 + 13), (125000, 16), jnp.float32)
        tbl_14 = 0.05 * jax.random.normal(jax.random.fold_in(_tk, 500 + 14), (1000, 16), jnp.float32)
        tbl_15 = 0.05 * jax.random.normal(jax.random.fold_in(_tk, 500 + 15), (1250, 16), jnp.float32)
        tbl_16 = 0.05 * jax.random.normal(jax.random.fold_in(_tk, 500 + 16), (125000, 16), jnp.float32)
        tbl_17 = 0.05 * jax.random.normal(jax.random.fold_in(_tk, 500 + 17), (1000, 16), jnp.float32)
        tbl_18 = 0.05 * jax.random.normal(jax.random.fold_in(_tk, 500 + 18), (1250, 16), jnp.float32)
        tbl_19 = 0.05 * jax.random.normal(jax.random.fold_in(_tk, 500 + 19), (125000, 16), jnp.float32)
        tbl_20 = 0.05 * jax.random.normal(jax.random.fold_in(_tk, 500 + 20), (1000, 16), jnp.float32)
        tbl_21 = 0.05 * jax.random.normal(jax.random.fold_in(_tk, 500 + 21), (12500, 16), jnp.float32)
        tbl_22 = 0.05 * jax.random.normal(jax.random.fold_in(_tk, 500 + 22), (1000, 16), jnp.float32)
        tbl_23 = 0.05 * jax.random.normal(jax.random.fold_in(_tk, 500 + 23), (1250, 16), jnp.float32)
        tbl_24 = 0.05 * jax.random.normal(jax.random.fold_in(_tk, 500 + 24), (1250, 16), jnp.float32)
        tbl_25 = 0.05 * jax.random.normal(jax.random.fold_in(_tk, 500 + 25), (12500, 16), jnp.float32)
        tbl_26 = 0.05 * jax.random.normal(jax.random.fold_in(_tk, 500 + 26), (1250, 16), jnp.float32)
        tbl_27 = 0.05 * jax.random.normal(jax.random.fold_in(_tk, 500 + 27), (125000, 16), jnp.float32)
        tbl_28 = 0.05 * jax.random.normal(jax.random.fold_in(_tk, 500 + 28), (125000, 16), jnp.float32)
        tbl_29 = 0.05 * jax.random.normal(jax.random.fold_in(_tk, 500 + 29), (125000, 16), jnp.float32)
        tbl_30 = 0.05 * jax.random.normal(jax.random.fold_in(_tk, 500 + 30), (12500, 16), jnp.float32)
        tbl_31 = 0.05 * jax.random.normal(jax.random.fold_in(_tk, 500 + 31), (1250, 16), jnp.float32)
        tbl_32 = 0.05 * jax.random.normal(jax.random.fold_in(_tk, 500 + 32), (125000, 16), jnp.float32)
        tbl_33 = 0.05 * jax.random.normal(jax.random.fold_in(_tk, 500 + 33), (125000, 16), jnp.float32)
        tbl_34 = 0.05 * jax.random.normal(jax.random.fold_in(_tk, 500 + 34), (1000, 16), jnp.float32)
        tbl_35 = 0.05 * jax.random.normal(jax.random.fold_in(_tk, 500 + 35), (1000, 16), jnp.float32)
        tbl_36 = 0.05 * jax.random.normal(jax.random.fold_in(_tk, 500 + 36), (125000, 16), jnp.float32)
        tbl_37 = 0.05 * jax.random.normal(jax.random.fold_in(_tk, 500 + 37), (1250, 16), jnp.float32)
        tbl_38 = 0.05 * jax.random.normal(jax.random.fold_in(_tk, 500 + 38), (12500, 16), jnp.float32)
        _rk = jax.random.fold_in(_tk, 7)
        W_top1 = 0.0606339 * jax.random.normal(jax.random.fold_in(_tk, 801), (272, 512), jnp.float32)
        W_top2 = 0.0441942 * jax.random.normal(jax.random.fold_in(_tk, 802), (512, 256), jnp.float32)
        W_top3 = 0.0625 * jax.random.normal(jax.random.fold_in(_tk, 803), (256, 1), jnp.float32)
        b_top1 = jnp.zeros((512,), jnp.float32)
        b_top2 = jnp.zeros((256,), jnp.float32)
        return (dense_ctx, ids, tbl_0, tbl_1, tbl_2, tbl_3, tbl_4, tbl_5, tbl_6, tbl_7, tbl_8, tbl_9, tbl_10, tbl_11, tbl_12, tbl_13, tbl_14, tbl_15, tbl_16, tbl_17, tbl_18, tbl_19, tbl_20, tbl_21, tbl_22, tbl_23, tbl_24, tbl_25, tbl_26, tbl_27, tbl_28, tbl_29, tbl_30, tbl_31, tbl_32, tbl_33, tbl_34, tbl_35, tbl_36, tbl_37, tbl_38, W_top1, b_top1, W_top2, b_top2, W_top3)
    dense_ctx, ids, tbl_0, tbl_1, tbl_2, tbl_3, tbl_4, tbl_5, tbl_6, tbl_7, tbl_8, tbl_9, tbl_10, tbl_11, tbl_12, tbl_13, tbl_14, tbl_15, tbl_16, tbl_17, tbl_18, tbl_19, tbl_20, tbl_21, tbl_22, tbl_23, tbl_24, tbl_25, tbl_26, tbl_27, tbl_28, tbl_29, tbl_30, tbl_31, tbl_32, tbl_33, tbl_34, tbl_35, tbl_36, tbl_37, tbl_38, W_top1, b_top1, W_top2, b_top2, W_top3 = _rec_inputs()

    def _L0_rec_setup():
        import jax, jax.numpy as jnp
        import numpy as np
        F0 = 39
        CIN_SIZES = [128, 128, 128]
        B, D = (512, 16)

        def _cin_forward(x, weights, biases):
            x0 = x
            xk = x
            fields = [F0] + CIN_SIZES
            outs = []
            for idx, s in enumerate(CIN_SIZES):
                fk = fields[idx]
                w = weights[idx].reshape(F0, fk, s)
                out = jnp.einsum('bid,bjd,ijs->bsd', x0, xk, w) + biases[idx][None, :, None]
                outs.append(out)
                xk = out
            res = jnp.concatenate(outs[1:], axis=1)
            return jnp.sum(res, axis=-1)
        key = jax.random.key(seed)
        ks = jax.random.split(key, 7)
        fields = [F0] + CIN_SIZES
        inp = {'x': jax.random.normal(ks[0], (B, F0, D), dtype=jnp.float32)}
        for i, s in enumerate(CIN_SIZES):
            m = fields[i] * F0
            inp[f'w{i}'] = jax.random.normal(ks[1 + 2 * i], (m, s), dtype=jnp.float32) * (2.0 / (m + s)) ** 0.5
            inp[f'b{i}'] = jax.random.normal(ks[2 + 2 * i], (s,), dtype=jnp.float32) * 0.02
        return inp
    _L0_rec_all = _L0_rec_setup()
    _L0_rec_in = {k: v for k, v in _L0_rec_all.items() if k in ('w0', 'b0', 'w1', 'b1', 'w2', 'b2')}
    del _L0_rec_all
    return {'dense_ctx': dense_ctx, 'ids': ids, 'tbl_0': tbl_0, 'tbl_1': tbl_1, 'tbl_2': tbl_2, 'tbl_3': tbl_3, 'tbl_4': tbl_4, 'tbl_5': tbl_5, 'tbl_6': tbl_6, 'tbl_7': tbl_7, 'tbl_8': tbl_8, 'tbl_9': tbl_9, 'tbl_10': tbl_10, 'tbl_11': tbl_11, 'tbl_12': tbl_12, 'tbl_13': tbl_13, 'tbl_14': tbl_14, 'tbl_15': tbl_15, 'tbl_16': tbl_16, 'tbl_17': tbl_17, 'tbl_18': tbl_18, 'tbl_19': tbl_19, 'tbl_20': tbl_20, 'tbl_21': tbl_21, 'tbl_22': tbl_22, 'tbl_23': tbl_23, 'tbl_24': tbl_24, 'tbl_25': tbl_25, 'tbl_26': tbl_26, 'tbl_27': tbl_27, 'tbl_28': tbl_28, 'tbl_29': tbl_29, 'tbl_30': tbl_30, 'tbl_31': tbl_31, 'tbl_32': tbl_32, 'tbl_33': tbl_33, 'tbl_34': tbl_34, 'tbl_35': tbl_35, 'tbl_36': tbl_36, 'tbl_37': tbl_37, 'tbl_38': tbl_38, 'W_top1': W_top1, 'b_top1': b_top1, 'W_top2': W_top2, 'b_top2': b_top2, 'W_top3': W_top3, 'L0_rec_w0': _L0_rec_in['w0'], 'L0_rec_b0': _L0_rec_in['b0'], 'L0_rec_w1': _L0_rec_in['w1'], 'L0_rec_b1': _L0_rec_in['b1'], 'L0_rec_w2': _L0_rec_in['w2'], 'L0_rec_b2': _L0_rec_in['b2']}

def reference(dense_ctx, ids, tbl_0, tbl_1, tbl_2, tbl_3, tbl_4, tbl_5, tbl_6, tbl_7, tbl_8, tbl_9, tbl_10, tbl_11, tbl_12, tbl_13, tbl_14, tbl_15, tbl_16, tbl_17, tbl_18, tbl_19, tbl_20, tbl_21, tbl_22, tbl_23, tbl_24, tbl_25, tbl_26, tbl_27, tbl_28, tbl_29, tbl_30, tbl_31, tbl_32, tbl_33, tbl_34, tbl_35, tbl_36, tbl_37, tbl_38, W_top1, b_top1, W_top2, b_top2, W_top3, L0_rec_w0, L0_rec_b0, L0_rec_w1, L0_rec_b1, L0_rec_w2, L0_rec_b2):
    import jax
    import jax.numpy as jnp

    def _L0_rec_ref(x, w0, b0, w1, b1, w2, b2):
        import jax, jax.numpy as jnp
        import numpy as np
        F0 = 39
        CIN_SIZES = [128, 128, 128]
        B, D = (512, 16)

        def _cin_forward(x, weights, biases):
            x0 = x
            xk = x
            fields = [F0] + CIN_SIZES
            outs = []
            for idx, s in enumerate(CIN_SIZES):
                fk = fields[idx]
                w = weights[idx].reshape(F0, fk, s)
                out = jnp.einsum('bid,bjd,ijs->bsd', x0, xk, w) + biases[idx][None, :, None]
                outs.append(out)
                xk = out
            res = jnp.concatenate(outs[1:], axis=1)
            return jnp.sum(res, axis=-1)
        return _cin_forward(x, [w0, w1, w2], [b0, b1, b2])
    e = jnp.stack([tbl_0[ids[:, 0]], tbl_1[ids[:, 1]], tbl_2[ids[:, 2]], tbl_3[ids[:, 3]], tbl_4[ids[:, 4]], tbl_5[ids[:, 5]], tbl_6[ids[:, 6]], tbl_7[ids[:, 7]], tbl_8[ids[:, 8]], tbl_9[ids[:, 9]], tbl_10[ids[:, 10]], tbl_11[ids[:, 11]], tbl_12[ids[:, 12]], tbl_13[ids[:, 13]], tbl_14[ids[:, 14]], tbl_15[ids[:, 15]], tbl_16[ids[:, 16]], tbl_17[ids[:, 17]], tbl_18[ids[:, 18]], tbl_19[ids[:, 19]], tbl_20[ids[:, 20]], tbl_21[ids[:, 21]], tbl_22[ids[:, 22]], tbl_23[ids[:, 23]], tbl_24[ids[:, 24]], tbl_25[ids[:, 25]], tbl_26[ids[:, 26]], tbl_27[ids[:, 27]], tbl_28[ids[:, 28]], tbl_29[ids[:, 29]], tbl_30[ids[:, 30]], tbl_31[ids[:, 31]], tbl_32[ids[:, 32]], tbl_33[ids[:, 33]], tbl_34[ids[:, 34]], tbl_35[ids[:, 35]], tbl_36[ids[:, 36]], tbl_37[ids[:, 37]], tbl_38[ids[:, 38]]], axis=1)
    z = _L0_rec_ref(e, L0_rec_w0, L0_rec_b0, L0_rec_w1, L0_rec_b1, L0_rec_w2, L0_rec_b2)
    z = z.reshape(z.shape[0], -1)
    h = jnp.concatenate([z, dense_ctx], axis=1)
    h = jnp.maximum(h @ W_top1 + b_top1, 0.0)
    h = jnp.maximum(h @ W_top2 + b_top2, 0.0)
    y = h @ W_top3
    return y

_drawn_inputs = setup_inputs


def setup_inputs(seed=0):
    import zlib

    import numpy as np

    out = dict(_drawn_inputs(seed))
    spreads = {'b_top1': (0.0, 0.8), 'b_top2': (0.0, 0.635)}
    factors = {'tbl_0': 8.0,
     'tbl_1': 8.0,
     'tbl_2': 8.0,
     'tbl_3': 8.0,
     'tbl_4': 8.0,
     'tbl_5': 8.0,
     'tbl_6': 8.0,
     'tbl_7': 8.0,
     'tbl_8': 8.0,
     'tbl_9': 8.0,
     'tbl_10': 8.0,
     'tbl_11': 8.0,
     'tbl_12': 8.0,
     'tbl_13': 8.0,
     'tbl_14': 8.0,
     'tbl_15': 8.0,
     'tbl_16': 8.0,
     'tbl_17': 8.0,
     'tbl_18': 8.0,
     'tbl_19': 8.0,
     'tbl_20': 8.0,
     'tbl_21': 8.0,
     'tbl_22': 8.0,
     'tbl_23': 8.0,
     'tbl_24': 8.0,
     'tbl_25': 8.0,
     'tbl_26': 8.0,
     'tbl_27': 8.0,
     'tbl_28': 8.0,
     'tbl_29': 8.0,
     'tbl_30': 8.0,
     'tbl_31': 8.0,
     'tbl_32': 8.0,
     'tbl_33': 8.0,
     'tbl_34': 8.0,
     'tbl_35': 8.0,
     'tbl_36': 8.0,
     'tbl_37': 8.0,
     'tbl_38': 8.0,
     'L0_rec_w0': 8.0,
     'L0_rec_b0': 3.321,
     'L0_rec_w1': 3.526,
     'L0_rec_w2': 2.825,
     'dense_ctx': 3.196,
     'L0_rec_b1': 3.655,
     'L0_rec_b2': 3.792}
    for name, (base, spread) in spreads.items():
        noise = np.random.default_rng([zlib.crc32(name.encode()), seed]).standard_normal(out[name].shape)
        drawn = base * np.exp(spread * noise) if base else spread * noise
        out[name] = jnp.asarray(drawn.astype(out[name].dtype))
    for name, factor in factors.items():
        out[name] = (out[name] * factor).astype(out[name].dtype)
    return out
```

```python
from contextlib import ExitStack

import numpy as np

import concourse.bass as bass
from concourse import mybir

ALU = mybir.AluOpType
ACT = mybir.ActivationFunctionType
F32 = mybir.dt.float32
F32R = mybir.dt.float32r
I32 = mybir.dt.int32

P = 128
F = 39
D = 16
S = 128
BATCH = 1024
POINTS = BATCH * D
BLOCK_SAMPLES = P // D
QBLOCKS = 4
QPOINTS = QBLOCKS * P
QUADS = POINTS // QPOINTS
QSAMPLES = QBLOCKS * BLOCK_SAMPLES
SEGQ = 8
SEGMENTS = QUADS // SEGQ
SEGB = SEGQ * QSAMPLES
DISTS = F // 2 + 1
DT = 3
TILES = -(-DISTS // DT)
ROWS = DT * F
LAST_ROWS = (DISTS - (TILES - 1) * DT) * F
GROUPS = 10
GW = 4 * S
FX = F + 1
RING = 5
HALF = 2
LROWS = 2 * F
LOOKUPS = HALF * BLOCK_SAMPLES
H1, H2 = 512, 256

ACT_GROUPS = (0, 2, 4, 5, 7, 9)
DVE_GROUPS = {1: 0, 3: 2, 6: 5, 8: 7}
SLOT = {0: 0, 4: 1, 2: 2, 5: 3, 7: 4, 9: 5}
NA, ND, SLOTS = len(ACT_GROUPS), len(DVE_GROUPS), len(SLOT)
CHAIN = 5
XD_AHEAD = QBLOCKS


def bass_dlrm_cin_tower(nc, t):
    with ExitStack() as ctx:
        def sb(name, shape, dt=F32):
            return ctx.enter_context(nc.sbuf_tensor(name, shape, dt))

        def psum(name, shape):
            return ctx.enter_context(nc.psum_tensor(name, shape, F32))

        def sem(name):
            return ctx.enter_context(nc.semaphore(name))

        ident = sb("ident", [P, P])
        mask = sb("mask", [P, BLOCK_SAMPLES])
        idx = sb("idx", [LROWS, QUADS * LOOKUPS], I32)
        idx_raw = sb("idx_raw", [LROWS, QUADS * LOOKUPS], I32)
        idx_now = sb("idx_now", [LROWS, LOOKUPS], I32)
        base = sb("base", [LROWS, 1])
        looked = sb("looked", [LROWS, HALF, P])
        fields = sb("fields", [ROWS, QPOINTS])
        pairs = sb("pairs", [P, TILES, QPOINTS])
        w0 = sb("w0", [ROWS, TILES, S])
        w0t = sb("w0t", [ROWS, TILES, S])
        w1h = sb("w1h", [P, F * S], F32R)
        w1l = sb("w1l", [P, F * S], F32R)
        w2 = sb("w2", [P, F, S])
        b0 = sb("b0", [P, 1])
        b2 = sb("b2", [P, 1])
        b2x = sb("b2x", [P, 1])
        x = sb("x", [P, QBLOCKS, FX])
        v32 = sb("v32", [P, QPOINTS])
        vh = sb("vh", [P, QPOINTS], F32R)
        vl = sb("vl", [P, QPOINTS], F32R)
        m = sb("m", [P, 2, SLOTS, GW])
        r = sb("r", [P, 2, SLOTS // 2, GW])
        y = sb("y", [P, 2, S])
        xd = sb("xd", [P, XD_AHEAD, FX, BLOCK_SAMPLES])
        g = sb("g", [P, FX, SEGB])
        z1 = sb("z1", [P, BATCH])
        z2 = sb("z2", [P, BATCH])
        bt1 = sb("bt1", [P, H1 // P])
        bt2 = sb("bt2", [P, H2 // P])
        wt3 = sb("wt3", [P, H2 // P])
        w1raw = g[:].rearrange("p i b -> p (i b)")[:, 0:F * S]
        idx_f = r[0:LROWS, 0, 0, :]
        wt1 = pairs[:, 0:2, :]
        wt2 = pairs[:, 2:4, :].rearrange("p a (c n) -> p (a c) n", n=H2)
        wt1d = pairs[0:D, 4, :]
        dense = pairs[0:D, 5:7, :]
        hidden = m[:].rearrange("p a c n -> p (a c) n")
        h1 = hidden[:, 0:8, :].rearrange("p (a f) n -> p a f n", a=2)
        h2 = hidden[:, 8:12, :].rearrange("p (a f) n -> p a f n", a=2)
        out_row = r[0:1, 0, 0:2, :]

        pt = psum("pt", [P, RING, GW])
        pv = psum("pv", [P, QPOINTS])
        pg = psum("pg", [P, GW])
        px = psum("px", [P, GW])
        pxt = px[:, 0:QBLOCKS * F].rearrange("p (c i) -> p c i", i=F)
        pz = px[:, SEGB:2 * SEGB]

        idx_in = sem("idx_in")
        consts_in = sem("consts_in")
        w0_in = sem("w0_in")
        w1_in = sem("w1_in")
        w2_in = sem("w2_in")
        mlp_in = sem("mlp_in")
        prep = sem("prep")
        idx_ready = sem("idx_ready")
        w0_ready = sem("w0_ready")
        w1h_ready = sem("w1h_ready")
        w1l_ready = sem("w1l_ready")
        b2_ready = sem("b2_ready")
        idx_staged = sem("idx_staged")
        looked_up = sem("looked_up")
        xt_stored = sem("xt_stored")
        fields_in = sem("fields_in")
        pairs_in = [sem(f"pairs_in{i}") for i in range(TILES)]
        pairs_ready = sem("pairs_ready")
        pairs_used = sem("pairs_used")
        xt_turned = sem("xt_turned")
        x_one = sem("x_one")
        x_ready = sem("x_ready")
        vh_ready = sem("vh_ready")
        v32_ready = sem("v32_ready")
        vl_ready = sem("vl_ready")
        t_ready = sem("t_ready")
        act_scaled = sem("act_scaled")
        dve_scaled = sem("dve_scaled")
        pool_added = sem("pool_added")
        chain = sem("chain")
        xd_ready = sem("xd_ready")
        g_made = sem("g_made")
        g_kept = sem("g_kept")
        l2_done = sem("l2_done")
        z_kept = sem("z_kept")
        z1_kept = sem("z1_kept")
        h_made = sem("h_made")
        h_kept = sem("h_kept")
        out_done = sem("out_done")

        xt_dram = t["xt"]

        block = ctx.enter_context(nc.Block())

        @block.sync
        def _(sp):
            sp.dma_start(idx_raw[:], t["ids"]).then_inc(idx_in, 16)
            sp.dma_start(base[:], t["base"]).then_inc(idx_in, 16)
            sp.dma_start(w0[:], t["w0"]).then_inc(w0_in, 16)
            sp.dma_start(w0t[:], t["w0t"]).then_inc(w0_in, 16)
            sp.dma_start(ident[:], t["ident"]).then_inc(consts_in, 16)
            sp.dma_start(mask[:], t["mask"]).then_inc(consts_in, 16)
            sp.dma_start(b0[:], t["b0"]).then_inc(consts_in, 16)
            sp.dma_start(b2[:], t["b2"]).then_inc(consts_in, 16)
            sp.dma_start(w1raw.rearrange("p (i s) -> p i s", s=S), t["w1"].rearrange("(i j) s -> j i s", j=S)).then_inc(w1_in, 16)
            for half in range(2):
                sp.dma_start(m[:, half, SLOT[GROUPS - 1], 3 * S:4 * S], t["b1"].partition_broadcast(P)).then_inc(consts_in, 16)

            def store(q):
                sp.wait_ge(looked_up, (q + 1) * (16 * LOOKUPS))
                for blk in range(2):
                    src = looked[blk * F:(blk + 1) * F, :, :]
                    for copy in range(2):
                        dst = xt_dram[copy * F:(copy + 1) * F, bass.ds(q * QPOINTS, QPOINTS)]
                        dst = dst.rearrange("f (h b n) -> f h b n", h=HALF, b=2)[:, :, blk, :]
                        sp.dma_start(dst, src).then_inc(xt_stored, 16)

            def load(q):
                sp.wait_ge(xt_stored, (q + 1) * 64)
                sp.wait_ge(pairs_ready, q * TILES + 1)
                sp.wait_ge(xt_turned, q + 1)
                cols = bass.ds(q * QPOINTS, QPOINTS)
                for rep in range(DT):
                    sp.dma_start(fields[rep * F:(rep + 1) * F, :], xt_dram[0:F, cols]).then_inc(fields_in, 16)
                for tile in range(TILES):
                    sp.wait_ge(pairs_used, q * TILES + tile + 1)
                    for kk in range(DT if tile < TILES - 1 else LAST_ROWS // F):
                        k = tile * DT + kk
                        sp.dma_start(pairs[kk * F:(kk + 1) * F, tile, :], xt_dram[k:k + F, cols]).then_inc(pairs_in[tile], 16)

            store(0)
            sp.dma_start(w2[:], t["w2"].rearrange("(i j) s -> j i s", j=S)).then_inc(w2_in, 16)
            sp.dma_start(bt1[:], t["bt1"]).then_inc(mlp_in, 16)
            sp.dma_start(bt2[:], t["bt2"]).then_inc(mlp_in, 16)
            sp.dma_start(wt3[:], t["wt3"]).then_inc(mlp_in, 16)
            with sp.Fori(0, QUADS - 1) as q:
                load(q)
                store(q + 1)
            load(QUADS - 1)
            sp.wait_ge(pairs_used, (QUADS + 1) * TILES)
            sp.dma_start(wt1, t["wt1"].rearrange("(c p) n -> p c n", p=P)).then_inc(mlp_in, 16)
            sp.dma_start(wt1d, t["wt1d"]).then_inc(mlp_in, 16)
            sp.dma_start(dense.rearrange("p a n -> p (a n)"), t["dense"]).then_inc(mlp_in, 16)
            sp.dma_start(wt2, t["wt2"].rearrange("(c p) n -> p c n", p=P)).then_inc(mlp_in, 16)
            sp.wait_ge(h_kept, 2 * (H1 + H2) // P + 2)
            sp.dma_start(t["out"], out_row.rearrange("p a n -> p (a n)")).then_inc(out_done, 16)
            sp.wait_ge(out_done, 16)

        @block.gpsimd
        def _(pool):
            pool.sem_inc(pool_added, 2)
            pool.wait_ge(idx_ready, 1)

            def stage(q, first=False):
                if not first:
                    pool.wait_ge(xt_stored, q * 64)
                nc.gpsimd.tensor_copy(idx_now[:], idx[:, bass.ds(q * LOOKUPS, LOOKUPS)]).then_inc(idx_staged, 1)

            def lookups(which):
                for n in which:
                    h, c = divmod(n, BLOCK_SAMPLES)
                    nc.gpsimd.indirect_dma_start(
                        out=looked[:, h, c * D:(c + 1) * D], out_offset=None, in_=t["tables"],
                        in_offset=bass.IndirectOffsetOnAxis(ap=idx_now[:, n:n + 1], axis=0),
                    ).then_inc(looked_up, 16)

            def diagonal(q, c):
                b = q * QBLOCKS + c
                pool.wait_ge(x_ready, q * 2 + (3 if c < 3 else 4))
                pool.wait_ge(g_made, b + 1)
                nc.gpsimd.tensor_tensor(
                    xd[:, c, :, :], x[:, c, :].unsqueeze(2).to_broadcast([P, FX, BLOCK_SAMPLES]),
                    mask[:].unsqueeze(1).to_broadcast([P, FX, BLOCK_SAMPLES]), ALU.mult).then_inc(xd_ready, 1)

            def add(q, c):
                par, b = c % 2, q * QBLOCKS + c
                pool.wait_ge(act_scaled, b * NA + NA + 4)
                pool.wait_ge(dve_scaled, b * ND + ND + 3)
                pool.wait_ge(chain, b * CHAIN + CHAIN)
                nc.gpsimd.tensor_tensor(r[:, par, 0:2, :], m[:, par, 0:2, :], m[:, par, 2:4, :], ALU.add).then_inc(pool_added, 1)

            for q in range(3):
                stage(q, first=(q == 0))
                pool.wait_ge(idx_staged, q + 1)
                lookups(range(LOOKUPS))
            pool.wait_ge(consts_in, 96)
            pool.wait_ge(x_one, 1)

            def quad(q, look):
                if look:
                    stage(q + 3)
                for c in range(QBLOCKS):
                    diagonal(q, c)
                    if look and c == 0:
                        pool.wait_ge(idx_staged, q + 4)
                    add(q, c)
                    if look:
                        lookups(range(4 * c, 4 * c + 4))

            with pool.Fori(0, QUADS - 3) as q:
                quad(q, True)
            with pool.Fori(QUADS - 3, QUADS) as q:
                quad(q, False)

        @block.tensor
        def _(pe):
            pe.sem_inc(g_made, XD_AHEAD)
            pe.sem_inc(pairs_used, TILES)
            pe.sem_inc(xt_turned, 1)

            def layer0(q, between=None):
                pe.wait_ge(fields_in, (q + 1) * 16 * DT)
                pe.wait_ge(x_ready, q * 2 + 2)
                for c in range(QBLOCKS):
                    mm = pe.transpose(px[:, c * F:c * F + ROWS], fields[:, c * P:(c + 1) * P], ident[0:ROWS, 0:ROWS])
                mm.then_inc(xt_turned, 1)
                pe.wait_ge(v32_ready, q * 2 + 2)
                pe.wait_ge(vh_ready, q * 2 + 2)
                for tile in range(TILES):
                    if tile == 3 and between:
                        between()
                    rows = ROWS if tile < TILES - 1 else LAST_ROWS
                    pe.wait_ge(pairs_ready, q * TILES + tile + 2)
                    mm = pe.matmul(pv[:, :], w0[0:rows, tile, :], pairs[0:rows, tile, :],
                                   start=(tile == 0), stop=(tile == TILES - 1))
                    mm.then_inc(pairs_used, 1)

            def layer1(q, c, between=None):
                b = q * QBLOCKS + c
                pe.wait_ge(vh_ready, q * 2 + (3 if c < 3 else 4))
                pe.wait_ge(vl_ready, q * 2 + (1 if c < 3 else 2))
                pts = slice(c * P, (c + 1) * P)
                for n in range(GROUPS):
                    if n == RING and between:
                        between()
                    last = (n + RING) % GROUPS
                    before = b if n >= RING else b - 1
                    if last in ACT_GROUPS:
                        pe.wait_ge(act_scaled, before * NA + NA + ACT_GROUPS.index(last) + 1)
                    else:
                        pe.wait_ge(dve_scaled, before * ND + ND + list(DVE_GROUPS).index(last) + 1)
                    cols = slice(n * GW, min((n + 1) * GW, F * S))
                    w = cols.stop - cols.start
                    out = pt[:, n % RING, 0:w]
                    pe.matmul(out, vh[:, pts], w1h[:, cols], start=True, stop=False)
                    pe.matmul(out, vh[:, pts], w1l[:, cols], start=False, stop=False)
                    pe.matmul(out, vl[:, pts], w1h[:, cols], start=False, stop=True).then_inc(t_ready, 1)

            def gram(q, c):
                par, b = c % 2, q * QBLOCKS + c
                pe.wait_ge(chain, b * CHAIN + 3 * CHAIN)
                pe.wait_ge(xd_ready, b + 1)
                pe.wait_ge(g_kept, b + 1)
                pe.matmul(pg[:, 0:FX * BLOCK_SAMPLES], y[:, par, :],
                          xd[:, c, :, :].rearrange("p i b -> p (i b)"), start=True, stop=True).then_inc(g_made, 1)

            def layer2(seg):
                pe.wait_ge(w2_in, 16)
                pe.wait_ge(g_kept, (seg + 1) * (SEGQ * QBLOCKS) + 1)
                pe.wait_ge(z_kept, seg + 1)
                for i in range(F):
                    mm = pe.matmul(pz, w2[:, i, :], g[:, i, :], start=(i == 0), stop=(i == F - 1))
                mm.then_inc(l2_done, 1)

            def quad(q, more):
                layer1(q, 2, lambda: gram(q, 0))
                if more:
                    layer0(q + 1, lambda: gram(q, 1))
                    layer1(q, 3, lambda: gram(q, 2))
                    layer1(q + 1, 0)
                    layer1(q + 1, 1, lambda: gram(q, 3))
                else:
                    layer1(q, 3, lambda: gram(q, 1))
                    gram(q, 2)
                    gram(q, 3)

            pe.wait_ge(consts_in, 96)
            pe.wait_ge(w0_ready, 1)
            layer0(0)
            pe.wait_ge(w1h_ready, 1)
            pe.wait_ge(w1l_ready, 1)
            layer1(0, 0)
            layer1(0, 1)
            with pe.Fori(0, SEGMENTS - 1) as seg:
                with pe.Fori(0, SEGQ) as k:
                    quad(seg * SEGQ + k, True)
                layer2(seg)
            with pe.Fori(QUADS - SEGQ, QUADS - 1) as q:
                quad(q, True)
            quad(QUADS - 1, False)
            layer2(SEGMENTS - 1)

            pe.wait_ge(mlp_in, 7 * 16)
            pe.wait_ge(z_kept, SEGMENTS + 1)
            pe.wait_ge(z1_kept, SEGMENTS)
            for half in range(2):
                cols = slice(half * 512, (half + 1) * 512)
                for f in range(H1 // P):
                    out = pt[:, f, :]
                    fs = slice(f * P, (f + 1) * P)
                    if half:
                        pe.wait_ge(h_kept, f + 1)
                    pe.matmul(out, wt1[:, 0, fs], z1[:, cols], start=True, stop=False)
                    pe.matmul(out, wt1[:, 1, fs], z2[:, cols], start=False, stop=False)
                    pe.matmul(out, wt1d[:, fs], dense[:, half, :], start=False, stop=True).then_inc(h_made, 1)
            kept = 2 * H1 // P
            for half in range(2):
                for f in range(H2 // P):
                    pe.wait_ge(h_kept, kept)
                    out = pt[:, 2 * half + f, :]
                    for c in range(H1 // P):
                        mm = pe.matmul(out, wt2[:, c, f * P:(f + 1) * P], h1[:, half, c, :],
                                       start=(c == 0), stop=(c == H1 // P - 1))
                    mm.then_inc(h_made, 1)
            kept += 2 * H2 // P
            for half in range(2):
                pe.wait_ge(h_kept, kept)
                out = (pv if half else pg)[0:1, :]
                for c in range(H2 // P):
                    mm = pe.matmul(out, wt3[:, c:c + 1], h2[:, half, c, :], start=(c == 0), stop=(c == H2 // P - 1))
                mm.then_inc(h_made, 1)

        @block.scalar
        def _(act):
            act.sem_inc(act_scaled, NA)
            act.sem_inc(g_kept, 1)
            act.sem_inc(z_kept, 1)
            act.sem_inc(x_ready, 2)
            act.sem_inc(v32_ready, 2)
            act.sem_inc(vh_ready, 2)

            act.wait_ge(consts_in, 96)
            nc.scalar.activation(b2x[:], b2[:], ACT.Copy, scale=float(D)).then_inc(b2_ready, 1)
            act.wait_ge(w1_in, 16)
            nc.scalar.activation(w1h[:], w1raw, ACT.Copy).then_inc(w1h_ready, 1)

            def keep(q, part, first=False):
                blocks = slice(0, 3) if part == 0 else slice(3, 4)
                pts = slice(blocks.start * P, blocks.stop * P)
                before = q * QBLOCKS - (1 if part == 0 else 0)
                act.wait_ge(xt_turned, q + 2)
                if not first:
                    act.wait_ge(dve_scaled, before * ND + ND)
                    act.wait_ge(xd_ready, before)
                    act.wait_ge(act_scaled, before * NA + NA)
                nc.scalar.activation(x[:, blocks, 0:F], pxt[:, blocks, :], ACT.Copy).then_inc(x_ready, 1)
                act.wait_ge(pairs_used, (q + 2) * TILES)
                if not first:
                    act.wait_ge(t_ready, before * GROUPS)
                    act.wait_ge(vl_ready, q * 2)
                nc.scalar.activation(vh[:, pts], pv[:, pts], ACT.Identity, bias=b0[:, 0:1]).then_inc(vh_ready, 1)
                nc.scalar.activation(v32[:, pts], pv[:, pts], ACT.Identity, bias=b0[:, 0:1]).then_inc(v32_ready, 1)

            def scale(q, c):
                par, b = c % 2, q * QBLOCKS + c
                act.wait_ge(x_ready, q * 2 + (3 if c < 3 else 4))
                act.wait_ge(pool_added, b + 1)
                act.wait_ge(chain, b * CHAIN + 1)
                for n in ACT_GROUPS:
                    act.wait_ge(t_ready, b * GROUPS + n + 1)
                    fs = range(4 * n, min(4 * n + 4, F))
                    for i in fs:
                        s = slice((i % 4) * S, (i % 4 + 1) * S)
                        ins = nc.scalar.activation(m[:, par, SLOT[n], s], pt[:, n % RING, s], ACT.Copy, scale=x[:, c, i:i + 1])
                    ins.then_inc(act_scaled, 1)

            def keep_g(q, c, k):
                b = q * QBLOCKS + c
                act.wait_ge(g_made, b + XD_AHEAD + 1)
                nc.scalar.activation(g[:, :, bass.ds(k * QSAMPLES + c * BLOCK_SAMPLES, BLOCK_SAMPLES)],
                                     pg[:, 0:FX * BLOCK_SAMPLES].rearrange("p (i b) -> p i b", i=FX),
                                     ACT.Copy).then_inc(g_kept, 1)

            def quad(q, k, more):
                scale(q, 2)
                keep_g(q, 0, k)
                if more:
                    keep_g(q, 1, k)
                    keep(q + 1, 0)
                    scale(q, 3)
                    keep_g(q, 2, k)
                    keep(q + 1, 1)
                    scale(q + 1, 0)
                    scale(q + 1, 1)
                    keep_g(q, 3, k)
                else:
                    scale(q, 3)
                    keep_g(q, 1, k)
                    keep_g(q, 2, k)
                    keep_g(q, 3, k)

            def keep_z(seg):
                act.wait_ge(g_kept, (seg + 1) * (SEGQ * QBLOCKS) + 1)
                nc.scalar.activation(z1[:, bass.ds(seg * SEGB, SEGB)], g[:, F, :], ACT.Copy).then_inc(z1_kept, 1)
                act.wait_ge(l2_done, seg + 1)
                nc.scalar.activation(z2[:, bass.ds(seg * SEGB, SEGB)], pz, ACT.Identity, bias=b2x[:, 0:1]).then_inc(z_kept, 1)

            act.wait_ge(x_one, 1)
            keep(0, 0, first=True)
            keep(0, 1, first=True)
            act.wait_ge(b2_ready, 1)
            scale(0, 0)
            scale(0, 1)
            with act.Fori(0, SEGMENTS - 1) as seg:
                with act.Fori(0, SEGQ) as k:
                    quad(seg * SEGQ + k, k, True)
                keep_z(seg)
            with act.Fori(QUADS - SEGQ, QUADS - 1) as q:
                quad(q, q - (QUADS - SEGQ), True)
            quad(QUADS - 1, SEGQ - 1, False)
            keep_z(SEGMENTS - 1)

            act.wait_ge(mlp_in, 7 * 16)
            made = 0
            for layer, (hid, width, bias, bank) in enumerate(((h1, H1, bt1, 0), (h2, H2, bt2, 1))):
                for half in range(2):
                    for f in range(width // P):
                        made += 1
                        act.wait_ge(h_made, made)
                        src = pt[:, f if layer == 0 else 2 * half + f, :]
                        nc.scalar.activation(hid[:, half, f, :], src, ACT.Relu, bias=bias[:, f:f + 1]).then_inc(h_kept, 1)
            for half in range(2):
                act.wait_ge(h_made, made + 1 + half)
                nc.scalar.activation(out_row[:, half, :], (pv if half else pg)[0:1, :], ACT.Copy).then_inc(h_kept, 1)

        @block.vector
        def _(dve):
            dve.sem_inc(dve_scaled, ND)
            dve.sem_inc(chain, 2 * CHAIN)
            dve.sem_inc(pairs_ready, 1)
            nc.vector.memset(x[:, :, F:FX], 1.0).then_inc(x_one, 1)

            dve.wait_ge(idx_in, 32)
            nc.vector.tensor_copy(idx_f, idx_raw[:]).then_inc(prep, 1)
            dve.wait_ge(prep, 1)
            nc.vector.tensor_scalar(idx[:], idx_f, base[:, 0:1], None, ALU.add).then_inc(idx_ready, 1)
            dve.wait_ge(w0_in, 32)
            nc.vector.tensor_tensor(w0[:], w0[:], w0t[:], ALU.add).then_inc(w0_ready, 1)
            dve.wait_ge(w1h_ready, 1)
            nc.vector.tensor_tensor(w1l[:], w1raw, w1h[:].bitcast(F32), ALU.subtract).then_inc(w1l_ready, 1)

            def product(q, tile):
                n = DT if tile < TILES - 1 else LAST_ROWS // F
                dve.wait_ge(fields_in, (q + 1) * (16 * DT))
                dve.wait_ge(pairs_in[tile], (q + 1) * (16 * n))
                nc.vector.tensor_tensor(pairs[0:n * F, tile, :], pairs[0:n * F, tile, :], fields[0:n * F, :],
                                        ALU.mult).then_inc(pairs_ready, 1)

            def split(q, part):
                pts = slice(0, 3 * P) if part == 0 else slice(3 * P, 4 * P)
                dve.wait_ge(v32_ready, q * 2 + part + 3)
                nc.vector.tensor_tensor(vl[:, pts], v32[:, pts], vh[:, pts].bitcast(F32), ALU.subtract).then_inc(vl_ready, 1)

            def scale(q, c, j):
                par, b = c % 2, q * QBLOCKS + c
                n, onto = list(DVE_GROUPS.items())[j]
                if j == 0:
                    dve.wait_ge(x_ready, q * 2 + (3 if c < 3 else 4))
                dve.wait_ge(act_scaled, b * NA + NA + ACT_GROUPS.index(onto) + 1)
                dve.wait_ge(t_ready, b * GROUPS + n + 1)
                for i in range(4):
                    s = slice(i * S, (i + 1) * S)
                    ins = nc.vector.scalar_tensor_tensor(
                        out=m[:, par, SLOT[onto], s], in0=pt[:, n % RING, s], scalar=x[:, c, 4 * n + i:4 * n + i + 1],
                        in1=m[:, par, SLOT[onto], s], op0=ALU.mult, op1=ALU.add)
                ins.then_inc(dve_scaled, 1)

            def add(q, c, step):
                par, b = c % 2, q * QBLOCKS + c
                rr = r[:, par, :, :]
                if step == 0:
                    dve.wait_ge(act_scaled, b * NA + 2 * NA)
                    dve.wait_ge(dve_scaled, b * ND + 2 * ND)
                    out, a, o = rr[:, 2, :], m[:, par, 4, :], m[:, par, 5, :]
                elif step == 1:
                    dve.wait_ge(pool_added, b + 3)
                    out, a, o = rr[:, 0, :], rr[:, 0, :], rr[:, 1, :]
                else:
                    dve.wait_ge(chain, b * CHAIN + 2 * CHAIN + step)
                if step == 2:
                    out, a, o = rr[:, 0, :], rr[:, 0, :], rr[:, 2, :]
                if step == 3:
                    out, a, o = rr[:, 0, 0:2 * S], rr[:, 0, 0:2 * S], rr[:, 0, 2 * S:4 * S]
                if step == 4:
                    dve.wait_ge(g_made, b + XD_AHEAD - 1)
                    out, a, o = y[:, par, :], rr[:, 0, 0:S], rr[:, 0, S:2 * S]
                nc.vector.tensor_tensor(out, a, o, ALU.add).then_inc(chain, 1)

            def scale_and_add(q, c, q_before, c_before):
                for j in range(ND):
                    scale(q, c, j)
                    add(q_before, c_before, j)
                add(q_before, c_before, ND)

            def quad(q, more, products):
                scale_and_add(q, 2, q, 1)
                if more:
                    for step in range(CHAIN):
                        add(q, 2, step)
                    split(q + 1, 0)
                    for j in range(ND):
                        scale(q, 3, j)
                        if products:
                            for tile in range(2 * j, min(2 * j + 2, TILES)):
                                product(q + 2, tile)
                    split(q + 1, 1)
                    scale_and_add(q + 1, 0, q, 3)
                    scale_and_add(q + 1, 1, q + 1, 0)
                else:
                    scale_and_add(q, 3, q, 2)
                    for step in range(CHAIN):
                        add(q, 3, step)

            for tile in range(TILES):
                product(0, tile)
            split(0, 0)
            split(0, 1)
            dve.wait_ge(consts_in, 96)
            for j in range(ND):
                scale(0, 0, j)
            for tile in range(TILES):
                product(1, tile)
            scale_and_add(0, 1, 0, 0)
            with dve.Fori(0, QUADS - 2) as q:
                quad(q, True, True)
            quad(QUADS - 2, True, False)
            quad(QUADS - 1, False, False)


def _pair_rows():
    direct = -np.ones((DT, F, TILES), np.int64)
    swapped = direct.copy()
    for k in range(DISTS):
        tile, kk = divmod(k, DT)
        for i in range(F):
            j = (i + k) % F
            direct[kk, i, tile] = i * F + j
            if k:
                swapped[kk, i, tile] = j * F + i
    return direct.reshape(ROWS, TILES), swapped.reshape(ROWS, TILES)


def kernel(**inputs):
    import concourse.bacc as _bacc
    from concourse.bass_utils import run_bass_kernel_spmd as _run

    def at(name):
        return np.asarray(inputs[name])

    tables = [at(f"tbl_{f}") for f in range(F)]
    starts = np.cumsum([0] + [tb.shape[0] for tb in tables[:-1]])
    assert starts[-1] + tables[-1].shape[0] < 1 << 24
    w0 = at("L0_rec_w0")
    w0x = np.concatenate([w0, np.zeros((1, S), w0.dtype)])
    direct, swapped = _pair_rows()
    ids = at("ids").reshape(QUADS, HALF, 2, BLOCK_SAMPLES, F).transpose(2, 4, 0, 1, 3)
    arrays = {
        "tables": np.concatenate(tables),
        "ids": ids.reshape(LROWS, QUADS * LOOKUPS),
        "base": np.tile(starts, 2).astype(np.float32).reshape(LROWS, 1),
        "ident": np.eye(P, dtype=np.float32),
        "mask": np.repeat(np.eye(BLOCK_SAMPLES, dtype=np.float32), D, axis=0),
        "w0": w0x[direct],
        "w0t": w0x[swapped],
        "w1": at("L0_rec_w1"),
        "w2": at("L0_rec_w2"),
        "b0": at("L0_rec_b0").reshape(S, 1),
        "b1": at("L0_rec_b1").reshape(S),
        "b2": at("L0_rec_b2").reshape(S, 1),
        "dense": at("dense_ctx").T,
        "wt1": at("W_top1")[0:2 * S],
        "wt1d": at("W_top1")[2 * S:],
        "wt2": at("W_top2"),
        "wt3": at("W_top3").reshape(H2 // P, P).T,
        "bt1": at("b_top1").reshape(H1 // P, P).T,
        "bt2": at("b_top2").reshape(H2 // P, P).T,
    }
    arrays = {k: np.ascontiguousarray(a) for k, a in arrays.items()}
    nc = _bacc.Bacc("TRN2", target_bir_lowering=False, num_devices=1)
    t = {k: nc.dram_tensor(k + "_dram", a.shape, mybir.dt.from_np(a.dtype), kind="ExternalInput").ap()
         for k, a in arrays.items()}
    t["out"] = nc.dram_tensor("out_dram", (1, BATCH), F32, kind="ExternalOutput").ap()
    t["xt"] = nc.dram_tensor("xt_dram", (2 * F, POINTS), F32, kind="Internal").ap()
    bass_dlrm_cin_tower(nc, t)
    res = _run(nc, [{k + "_dram": a for k, a in arrays.items()}], core_ids=[0])
    return res.results[0]["out_dram"].reshape(BATCH, 1)
```

```python
from contextlib import ExitStack

import numpy as np

import concourse.bass as bass
from concourse import mybir

ALU = mybir.AluOpType
ACT = mybir.ActivationFunctionType
F32 = mybir.dt.float32
F32R = mybir.dt.float32r
I32 = mybir.dt.int32

P = 128
F = 39
D = 16
S = 128
BATCH = 1024
POINTS = BATCH * D
BLOCK_SAMPLES = P // D
QBLOCKS = 4
QPOINTS = QBLOCKS * P
QUADS = POINTS // QPOINTS
QSAMPLES = QBLOCKS * BLOCK_SAMPLES
SEGQ = 8
SEGMENTS = QUADS // SEGQ
SEGB = SEGQ * QSAMPLES
DISTS = F // 2 + 1
DT = 3
TILES = -(-DISTS // DT)
ROWS = DT * F
LAST_ROWS = (DISTS - (TILES - 1) * DT) * F
GROUPS = 10
GW = 4 * S
FX = F + 1
RING = 5
PARTS = P // F
LROWS = PARTS * F
LOOKUPS = -(-QSAMPLES // PARTS)
H1, H2 = 512, 256

ACT_GROUPS = (0, 2, 4, 5, 7, 9)
DVE_GROUPS = {1: 0, 3: 2, 6: 5, 8: 7}
SLOT = {0: 0, 4: 1, 2: 2, 5: 3, 7: 4, 9: 5}
NA, ND, SLOTS = len(ACT_GROUPS), len(DVE_GROUPS), len(SLOT)
STORED = 16 * 2 * PARTS
CHAIN = 4
LOOKS = (range(0), range(0, 2), range(2, 8), range(8, LOOKUPS))
EARLY = 5
XD_AHEAD = QBLOCKS


def bass_dlrm_cin_tower(nc, t):
    with ExitStack() as ctx:
        def sb(name, shape, dt=F32):
            return ctx.enter_context(nc.sbuf_tensor(name, shape, dt))

        def psum(name, shape):
            return ctx.enter_context(nc.psum_tensor(name, shape, F32))

        def sem(name):
            return ctx.enter_context(nc.semaphore(name))

        ident = sb("ident", [P, P])
        mask = sb("mask", [P, BLOCK_SAMPLES])
        idx = sb("idx", [LROWS, QUADS * LOOKUPS], I32)
        idx_raw = sb("idx_raw", [LROWS, QUADS * LOOKUPS], I32)
        idx_now = sb("idx_now", [LROWS, LOOKUPS], I32)
        base = sb("base", [LROWS, 1])
        looked = sb("looked", [LROWS, LOOKUPS, D])
        fields = sb("fields", [ROWS, QPOINTS])
        pairs = sb("pairs", [P, TILES, QPOINTS])
        w0 = sb("w0", [ROWS, TILES, S])
        w0t = sb("w0t", [ROWS, TILES, S])
        w1h = sb("w1h", [P, F * S], F32R)
        w1l = sb("w1l", [P, F * S], F32R)
        w2 = sb("w2", [P, F, S])
        b0 = sb("b0", [P, 1])
        b2 = sb("b2", [P, 1])
        b2x = sb("b2x", [P, 1])
        x = sb("x", [P, QBLOCKS, FX])
        vh = sb("vh", [P, QPOINTS], F32R)
        vl = sb("vl", [P, QPOINTS], F32R)
        m = sb("m", [P, 2, SLOTS, GW])
        r = sb("r", [P, 2, SLOTS // 2, GW])
        y = sb("y", [P, 2, S])
        xd = sb("xd", [P, XD_AHEAD, FX, BLOCK_SAMPLES])
        g = sb("g", [P, FX, SEGB])
        z1 = sb("z1", [P, BATCH])
        z2 = sb("z2", [P, BATCH])
        bt1 = sb("bt1", [P, H1 // P])
        bt2 = sb("bt2", [P, H2 // P])
        wt3 = sb("wt3", [P, H2 // P])
        w1raw = g[:].rearrange("p i b -> p (i b)")[:, 0:F * S]
        idx_f = r[0:LROWS, 0, 0, 0:QUADS * LOOKUPS]
        wt1 = pairs[:, 0:2, :]
        wt2 = pairs[:, 2:4, :].rearrange("p a (c n) -> p (a c) n", n=H2)
        wt1d = pairs[0:D, 4, :]
        dense = pairs[0:D, 5:7, :]
        hidden = m[:].rearrange("p a c n -> p (a c) n")
        h1 = hidden[:, 0:8, :].rearrange("p (a f) n -> p a f n", a=2)
        h2 = hidden[:, 8:12, :].rearrange("p (a f) n -> p a f n", a=2)
        out_row = r[0:1, 0, 0:2, :]

        pt = psum("pt", [P, RING, GW])
        pv = psum("pv", [P, QPOINTS])
        pg = psum("pg", [P, GW])
        px = psum("px", [P, GW])
        pxt = px[:, 0:QBLOCKS * F].rearrange("p (c i) -> p c i", i=F)
        pz = px[:, SEGB:2 * SEGB]

        idx_in = sem("idx_in")
        consts_in = sem("consts_in")
        w0_in = sem("w0_in")
        w1_in = sem("w1_in")
        w2_in = sem("w2_in")
        mlp_in = sem("mlp_in")
        prep = sem("prep")
        idx_ready = sem("idx_ready")
        w0_ready = sem("w0_ready")
        w1h_ready = sem("w1h_ready")
        w1l_ready = sem("w1l_ready")
        b2_ready = sem("b2_ready")
        idx_staged = sem("idx_staged")
        looked_up = sem("looked_up")
        xt_stored = sem("xt_stored")
        fields_in = sem("fields_in")
        pairs_in = [sem(f"pairs_in{i}") for i in range(TILES)]
        pairs_ready = sem("pairs_ready")
        pairs_used = sem("pairs_used")
        xt_turned = sem("xt_turned")
        x_one = sem("x_one")
        x_ready = sem("x_ready")
        vh_ready = sem("vh_ready")
        vl_ready = sem("vl_ready")
        t_ready = sem("t_ready")
        act_scaled = sem("act_scaled")
        dve_scaled = sem("dve_scaled")
        pool_added = sem("pool_added")
        chain = sem("chain")
        xd_ready = sem("xd_ready")
        g_made = sem("g_made")
        g_kept = sem("g_kept")
        l2_done = sem("l2_done")
        z_kept = sem("z_kept")
        z1_kept = sem("z1_kept")
        h_made = sem("h_made")
        h_kept = sem("h_kept")
        out_done = sem("out_done")

        xt_dram = t["xt"]

        block = ctx.enter_context(nc.Block())

        @block.sync
        def _(sp):
            sp.dma_start(idx_raw[:], t["ids"]).then_inc(idx_in, 16)
            sp.dma_start(base[:], t["base"]).then_inc(idx_in, 16)
            sp.dma_start(w0[:], t["w0"]).then_inc(w0_in, 16)
            sp.dma_start(w0t[:], t["w0t"]).then_inc(w0_in, 16)
            sp.dma_start(ident[:], t["ident"]).then_inc(consts_in, 16)
            sp.dma_start(mask[:], t["mask"]).then_inc(consts_in, 16)
            sp.dma_start(b0[:], t["b0"]).then_inc(consts_in, 16)
            sp.dma_start(b2[:], t["b2"]).then_inc(consts_in, 16)
            sp.dma_start(w1raw.rearrange("p (i s) -> p i s", s=S), t["w1"].rearrange("(i j) s -> j i s", j=S)).then_inc(w1_in, 16)
            for half in range(2):
                sp.dma_start(m[:, half, SLOT[GROUPS - 1], 3 * S:4 * S], t["b1"].partition_broadcast(P)).then_inc(consts_in, 16)

            def store(q):
                sp.wait_ge(looked_up, (q + 1) * (16 * LOOKUPS))
                for part in range(PARTS):
                    n = min(LOOKUPS, QSAMPLES - part * LOOKUPS)
                    src = looked[part * F:(part + 1) * F, 0:n, :].rearrange("f c d -> f (c d)")
                    for copy in range(2):
                        dst = xt_dram[copy * F:(copy + 1) * F, bass.ds(q * QPOINTS + part * (LOOKUPS * D), n * D)]
                        sp.dma_start(dst, src).then_inc(xt_stored, 16)

            def rows_of(q, first, step, n):
                return bass.AP(tensor=xt_dram.tensor, offset=q * QPOINTS + first * POINTS,
                               ap=[[step * POINTS, n], [POINTS, F], [1, QPOINTS]])

            def load(q):
                sp.wait_ge(xt_stored, (q + 1) * STORED)
                sp.wait_ge(pairs_ready, q * TILES + 1)
                sp.wait_ge(xt_turned, q + 1)
                sp.dma_start(fields[:], rows_of(q, 0, 0, DT)).then_inc(fields_in, 16)
                for tile in range(TILES):
                    sp.wait_ge(pairs_used, q * TILES + tile + 1)
                    n = DT if tile < TILES - 1 else LAST_ROWS // F
                    sp.dma_start(pairs[0:n * F, tile, :], rows_of(q, tile * DT, 1, n)).then_inc(pairs_in[tile], 16)

            store(0)
            load(0)
            store(1)
            sp.dma_start(w2[:], t["w2"].rearrange("(i j) s -> j i s", j=S)).then_inc(w2_in, 16)
            sp.dma_start(bt1[:], t["bt1"]).then_inc(mlp_in, 16)
            sp.dma_start(bt2[:], t["bt2"]).then_inc(mlp_in, 16)
            sp.dma_start(wt3[:], t["wt3"]).then_inc(mlp_in, 16)
            with sp.Fori(1, QUADS - 1) as q:
                load(q)
                store(q + 1)
            load(QUADS - 1)
            sp.wait_ge(pairs_used, (QUADS + 1) * TILES)
            sp.dma_start(wt1, t["wt1"].rearrange("(c p) n -> p c n", p=P)).then_inc(mlp_in, 16)
            sp.dma_start(wt1d, t["wt1d"]).then_inc(mlp_in, 16)
            sp.dma_start(dense.rearrange("p a n -> p (a n)"), t["dense"]).then_inc(mlp_in, 16)
            sp.dma_start(wt2, t["wt2"].rearrange("(c p) n -> p c n", p=P)).then_inc(mlp_in, 16)
            sp.wait_ge(h_kept, 2 * (H1 + H2) // P + 2)
            sp.dma_start(t["out"], out_row.rearrange("p a n -> p (a n)")).then_inc(out_done, 16)
            sp.wait_ge(out_done, 16)

        @block.gpsimd
        def _(pool):
            pool.sem_inc(pool_added, 4)
            pool.wait_ge(idx_ready, 1)

            def stage(q, first=False):
                if not first:
                    pool.wait_ge(xt_stored, q * STORED)
                nc.gpsimd.tensor_copy(idx_now[:], idx[:, bass.ds(q * LOOKUPS, LOOKUPS)]).then_inc(idx_staged, 1)

            def lookups(which):
                for n in which:
                    nc.gpsimd.indirect_dma_start(
                        out=looked[:, n, :], out_offset=None, in_=t["tables"],
                        in_offset=bass.IndirectOffsetOnAxis(ap=idx_now[:, n:n + 1], axis=0),
                    ).then_inc(looked_up, 16)

            def diagonal(q, c):
                b = q * QBLOCKS + c
                pool.wait_ge(x_ready, q * 2 + (3 if c < 3 else 4))
                pool.wait_ge(g_made, b + 1)
                nc.gpsimd.tensor_tensor(
                    xd[:, c, :, :], x[:, c, :].unsqueeze(2).to_broadcast([P, FX, BLOCK_SAMPLES]),
                    mask[:].unsqueeze(1).to_broadcast([P, FX, BLOCK_SAMPLES]), ALU.mult).then_inc(xd_ready, 1)

            def add(q, c):
                par, b = c % 2, q * QBLOCKS + c
                pool.wait_ge(act_scaled, b * NA + NA + 4)
                pool.wait_ge(dve_scaled, b * ND + ND + 3)
                pool.wait_ge(chain, b * CHAIN + 2)
                nc.gpsimd.tensor_tensor(r[:, par, 0:2, :], m[:, par, 0:2, :], m[:, par, 2:4, :], ALU.add).then_inc(pool_added, 1)
                pool.wait_ge(pool_added, b * 2 + 5)
                nc.gpsimd.tensor_tensor(r[:, par, 0, :], r[:, par, 0, :], r[:, par, 1, :], ALU.add).then_inc(pool_added, 1)

            for q in range(3):
                stage(q, first=(q == 0))
                pool.wait_ge(idx_staged, q + 1)
                lookups(range(LOOKUPS))
            pool.wait_ge(consts_in, 96)
            pool.wait_ge(x_one, 1)

            def quad(q, look):
                for c in range(QBLOCKS):
                    diagonal(q, c)
                    if look and c == 1:
                        pool.wait_ge(idx_staged, q + 4)
                    add(q, c)
                    if look and c == 0:
                        stage(q + 3)
                    if look:
                        lookups(LOOKS[c])

            with pool.Fori(0, QUADS - 3) as q:
                quad(q, True)
            with pool.Fori(QUADS - 3, QUADS) as q:
                quad(q, False)

        @block.tensor
        def _(pe):
            pe.sem_inc(g_made, XD_AHEAD)
            pe.sem_inc(pairs_used, TILES)
            pe.sem_inc(xt_turned, 1)

            def layer0(q, between=None):
                pe.wait_ge(fields_in, (q + 1) * 16)
                pe.wait_ge(x_ready, q * 2 + 2)
                for c in range(QBLOCKS):
                    n = ROWS if c == 0 else F
                    mm = pe.transpose(px[:, c * F:c * F + n], fields[0:n, c * P:(c + 1) * P], ident[0:n, 0:n])
                mm.then_inc(xt_turned, 1)
                pe.wait_ge(vl_ready, q * 2 + 2)
                for tile in range(TILES):
                    if tile == 3 and between:
                        between()
                    rows = ROWS if tile < TILES - 1 else LAST_ROWS
                    pe.wait_ge(pairs_ready, q * TILES + tile + 2)
                    mm = pe.matmul(pv[:, :], w0[0:rows, tile, :], pairs[0:rows, tile, :],
                                   start=(tile == 0), stop=(tile == TILES - 1))
                    mm.then_inc(pairs_used, 1)

            def layer1(q, c, between=None):
                b = q * QBLOCKS + c
                pe.wait_ge(vh_ready, q * 2 + (3 if c < 3 else 4))
                pe.wait_ge(vl_ready, q * 2 + (3 if c < 3 else 4))
                pts = slice(c * P, (c + 1) * P)
                for n in range(GROUPS):
                    if n == RING and between:
                        between()
                    last = (n + RING) % GROUPS
                    before = b if n >= RING else b - 1
                    if last in ACT_GROUPS:
                        pe.wait_ge(act_scaled, before * NA + NA + ACT_GROUPS.index(last) + 1)
                    else:
                        pe.wait_ge(dve_scaled, before * ND + ND + list(DVE_GROUPS).index(last) + 1)
                    cols = slice(n * GW, min((n + 1) * GW, F * S))
                    w = cols.stop - cols.start
                    out = pt[:, n % RING, 0:w]
                    pe.matmul(out, vh[:, pts], w1h[:, cols], start=True, stop=False)
                    pe.matmul(out, vh[:, pts], w1l[:, cols], start=False, stop=False)
                    pe.matmul(out, vl[:, pts], w1h[:, cols], start=False, stop=True).then_inc(t_ready, 1)

            def gram(q, c):
                par, b = c % 2, q * QBLOCKS + c
                pe.wait_ge(chain, b * CHAIN + 3 * CHAIN)
                pe.wait_ge(xd_ready, b + 1)
                pe.wait_ge(g_kept, b + 1)
                pe.matmul(pg[:, 0:FX * BLOCK_SAMPLES], y[:, par, :],
                          xd[:, c, :, :].rearrange("p i b -> p (i b)"), start=True, stop=True).then_inc(g_made, 1)

            def layer2(seg, more):
                pe.wait_ge(w2_in, 16)
                pe.wait_ge(g_kept, (seg + 1) * (SEGQ * QBLOCKS) + 1)
                pe.wait_ge(z_kept, seg + 1)
                if more:
                    pe.wait_ge(x_ready, (seg + 1) * (SEGQ * 2) + 4)
                for i in range(F):
                    mm = pe.matmul(pz, w2[:, i, :], g[:, i, :], start=(i == 0), stop=(i == F - 1))
                mm.then_inc(l2_done, 1)

            def hidden1(half):
                cols = slice(half * 512, (half + 1) * 512)
                for f in range(H1 // P):
                    out = pt[:, f, :]
                    fs = slice(f * P, (f + 1) * P)
                    if half:
                        pe.wait_ge(h_kept, f + 1)
                    pe.matmul(out, wt1[:, 0, fs], z1[:, cols], start=True, stop=False)
                    pe.matmul(out, wt1[:, 1, fs], z2[:, cols], start=False, stop=False)
                    pe.matmul(out, wt1d[:, fs], dense[:, half, :], start=False, stop=True).then_inc(h_made, 1)

            def quad(q, more):
                layer1(q, 2, lambda: gram(q, 0))
                if more:
                    layer0(q + 1, lambda: gram(q, 1))
                    layer1(q, 3, lambda: gram(q, 2))
                    layer1(q + 1, 0)
                    layer1(q + 1, 1, lambda: gram(q, 3))
                else:
                    layer1(q, 3, lambda: gram(q, 1))
                    gram(q, 2)
                    pe.wait_ge(mlp_in, 7 * 16)
                    pe.wait_ge(z_kept, SEGMENTS)
                    pe.wait_ge(z1_kept, SEGMENTS - 1)
                    pe.wait_ge(act_scaled, (QUADS * QBLOCKS + 1) * NA)
                    pe.wait_ge(dve_scaled, (QUADS * QBLOCKS + 1) * ND)
                    hidden1(0)
                    gram(q, 3)

            pe.wait_ge(consts_in, 96)
            pe.wait_ge(w0_ready, 1)
            layer0(0)
            pe.wait_ge(w1h_ready, 1)
            pe.wait_ge(w1l_ready, 1)
            layer1(0, 0)
            layer1(0, 1)
            with pe.Fori(0, SEGMENTS - 1) as seg:
                with pe.Fori(0, SEGQ) as k:
                    quad(seg * SEGQ + k, True)
                layer2(seg, True)
            with pe.Fori(QUADS - SEGQ, QUADS - 1) as q:
                quad(q, True)
            quad(QUADS - 1, False)
            layer2(SEGMENTS - 1, False)

            pe.wait_ge(z_kept, SEGMENTS + 1)
            pe.wait_ge(z1_kept, SEGMENTS)
            hidden1(1)
            kept = 2 * H1 // P
            for half in range(2):
                for f in range(H2 // P):
                    pe.wait_ge(h_kept, kept)
                    out = pt[:, 2 * half + f, :]
                    for c in range(H1 // P):
                        mm = pe.matmul(out, wt2[:, c, f * P:(f + 1) * P], h1[:, half, c, :],
                                       start=(c == 0), stop=(c == H1 // P - 1))
                    mm.then_inc(h_made, 1)
            kept += 2 * H2 // P
            for half in range(2):
                pe.wait_ge(h_kept, kept)
                out = (pv if half else pg)[0:1, :]
                for c in range(H2 // P):
                    mm = pe.matmul(out, wt3[:, c:c + 1], h2[:, half, c, :], start=(c == 0), stop=(c == H2 // P - 1))
                mm.then_inc(h_made, 1)

        @block.scalar
        def _(act):
            act.sem_inc(act_scaled, NA)
            act.sem_inc(g_kept, 1)
            act.sem_inc(z_kept, 1)
            act.sem_inc(x_ready, 2)
            act.sem_inc(vh_ready, 2)

            act.wait_ge(consts_in, 96)
            nc.scalar.activation(b2x[:], b2[:], ACT.Copy, scale=float(D)).then_inc(b2_ready, 1)
            act.wait_ge(w1_in, 16)
            nc.scalar.activation(w1h[:], w1raw, ACT.Copy).then_inc(w1h_ready, 1)

            def keep_x(q, part, first=False):
                blocks = slice(0, 3) if part == 0 else slice(3, 4)
                before = q * QBLOCKS - 1 + part
                act.wait_ge(xt_turned, q + 2)
                if not first:
                    act.wait_ge(dve_scaled, before * ND + ND)
                    act.wait_ge(xd_ready, before)
                    act.wait_ge(act_scaled, before * NA + NA)
                nc.scalar.activation(x[:, blocks, 0:F], pxt[:, blocks, :], ACT.Copy).then_inc(x_ready, 1)

            def keep_v(q, part, first=False):
                pts = slice(0, 3 * P) if part == 0 else slice(3 * P, 4 * P)
                before = q * QBLOCKS - 1 + part
                act.wait_ge(pairs_used, (q + 2) * TILES)
                if not first:
                    act.wait_ge(t_ready, before * GROUPS)
                act.wait_ge(vl_ready, q * 2 + part + 2)
                nc.scalar.activation(vh[:, pts], pv[:, pts], ACT.Identity, bias=b0[:, 0:1]).then_inc(vh_ready, 1)

            def scale(q, c, groups=ACT_GROUPS):
                par, b = c % 2, q * QBLOCKS + c
                if 0 in groups:
                    act.wait_ge(x_ready, q * 2 + (3 if c < 3 else 4))
                    act.wait_ge(pool_added, b * 2 + 1)
                    act.wait_ge(chain, b * CHAIN + 1)
                for n in groups:
                    act.wait_ge(t_ready, b * GROUPS + n + 1)
                    fs = range(4 * n, min(4 * n + 4, F))
                    for i in fs:
                        s = slice((i % 4) * S, (i % 4 + 1) * S)
                        ins = nc.scalar.activation(m[:, par, SLOT[n], s], pt[:, n % RING, s], ACT.Copy, scale=x[:, c, i:i + 1])
                    ins.then_inc(act_scaled, 1)

            def keep_g(q, c, k):
                b = q * QBLOCKS + c
                act.wait_ge(g_made, b + XD_AHEAD + 1)
                nc.scalar.activation(g[:, :, bass.ds(k * QSAMPLES + c * BLOCK_SAMPLES, BLOCK_SAMPLES)],
                                     pg[:, 0:FX * BLOCK_SAMPLES].rearrange("p (i b) -> p i b", i=FX),
                                     ACT.Copy).then_inc(g_kept, 1)

            made = [0]

            def keep_hidden(hid, bias, bank, half):
                for f in range(hid.shape[2]):
                    made[0] += 1
                    act.wait_ge(h_made, made[0])
                    nc.scalar.activation(hid[:, half, f, :], pt[:, bank + f, :], ACT.Relu, bias=bias[:, f:f + 1]).then_inc(h_kept, 1)

            def quad(q, k, more):
                scale(q, 2)
                keep_g(q, 0, k)
                if more:
                    keep_g(q, 1, k)
                    scale(q, 3, ACT_GROUPS[0:2])
                    keep_x(q + 1, 0)
                    keep_v(q + 1, 0)
                    scale(q, 3, ACT_GROUPS[2:])
                    keep_g(q, 2, k)
                    scale(q + 1, 0)
                    keep_x(q + 1, 1)
                    scale(q + 1, 1)
                    keep_g(q, 3, k)
                    keep_v(q + 1, 1)
                else:
                    scale(q, 3)
                    keep_g(q, 1, k)
                    keep_g(q, 2, k)
                    act.wait_ge(mlp_in, 7 * 16)
                    act.wait_ge(pool_added, QUADS * QBLOCKS * 2 + 2)
                    act.wait_ge(chain, (QUADS * QBLOCKS + 1) * CHAIN)
                    keep_hidden(h1, bt1, 0, 0)
                    keep_g(q, 3, k)

            def keep_z(seg):
                act.wait_ge(g_kept, (seg + 1) * (SEGQ * QBLOCKS) + 1)
                nc.scalar.activation(z1[:, bass.ds(seg * SEGB, SEGB)], g[:, F, :], ACT.Copy).then_inc(z1_kept, 1)
                act.wait_ge(l2_done, seg + 1)
                nc.scalar.activation(z2[:, bass.ds(seg * SEGB, SEGB)], pz, ACT.Identity, bias=b2x[:, 0:1]).then_inc(z_kept, 1)

            act.wait_ge(x_one, 1)
            for part in range(2):
                keep_x(0, part, first=True)
                keep_v(0, part, first=True)
            act.wait_ge(b2_ready, 1)
            scale(0, 0)
            scale(0, 1)
            with act.Fori(0, SEGMENTS - 1) as seg:
                with act.Fori(0, SEGQ) as k:
                    quad(seg * SEGQ + k, k, True)
                keep_z(seg)
            with act.Fori(QUADS - SEGQ, QUADS - 1) as q:
                quad(q, q - (QUADS - SEGQ), True)
            quad(QUADS - 1, SEGQ - 1, False)
            keep_z(SEGMENTS - 1)

            keep_hidden(h1, bt1, 0, 1)
            for half in range(2):
                keep_hidden(h2, bt2, 2 * half, half)
            for half in range(2):
                act.wait_ge(h_made, 2 * (H1 + H2) // P + 1 + half)
                nc.scalar.activation(out_row[:, half, :], (pv if half else pg)[0:1, :], ACT.Copy).then_inc(h_kept, 1)

        @block.vector
        def _(dve):
            dve.sem_inc(dve_scaled, ND)
            dve.sem_inc(chain, 2 * CHAIN)
            dve.sem_inc(pairs_ready, 1)
            dve.sem_inc(vl_ready, 2)
            nc.vector.memset(x[:, :, F:FX], 1.0).then_inc(x_one, 1)

            dve.wait_ge(idx_in, 32)
            nc.vector.tensor_copy(idx_f, idx_raw[:]).then_inc(prep, 1)
            dve.wait_ge(prep, 1)
            nc.vector.tensor_scalar(idx[:], idx_f, base[:, 0:1], None, ALU.add).then_inc(idx_ready, 1)
            dve.wait_ge(w0_in, 32)
            nc.vector.tensor_tensor(w0[:], w0[:], w0t[:], ALU.add).then_inc(w0_ready, 1)
            dve.wait_ge(w1h_ready, 1)
            nc.vector.tensor_tensor(w1l[:], w1raw, w1h[:].bitcast(F32), ALU.subtract).then_inc(w1l_ready, 1)

            def product(q, tile):
                n = DT if tile < TILES - 1 else LAST_ROWS // F
                dve.wait_ge(fields_in, (q + 1) * 16)
                dve.wait_ge(pairs_in[tile], (q + 1) * 16)
                nc.vector.tensor_tensor(pairs[0:n * F, tile, :], pairs[0:n * F, tile, :], fields[0:n * F, :],
                                        ALU.mult).then_inc(pairs_ready, 1)

            def split(q, part):
                pts = slice(0, 3 * P) if part == 0 else slice(3 * P, 4 * P)
                dve.wait_ge(vh_ready, q * 2 + part + 3)
                nc.vector.scalar_tensor_tensor(out=vl[:, pts], in0=pv[:, pts], scalar=b0[:, 0:1], in1=vh[:, pts].bitcast(F32),
                                               op0=ALU.add, op1=ALU.subtract).then_inc(vl_ready, 1)

            def scale(q, c, j):
                par, b = c % 2, q * QBLOCKS + c
                n, onto = list(DVE_GROUPS.items())[j]
                if j == 0:
                    dve.wait_ge(x_ready, q * 2 + (3 if c < 3 else 4))
                dve.wait_ge(act_scaled, b * NA + NA + ACT_GROUPS.index(onto) + 1)
                dve.wait_ge(t_ready, b * GROUPS + n + 1)
                for i in range(4):
                    s = slice(i * S, (i + 1) * S)
                    ins = nc.vector.scalar_tensor_tensor(
                        out=m[:, par, SLOT[onto], s], in0=pt[:, n % RING, s], scalar=x[:, c, 4 * n + i:4 * n + i + 1],
                        in1=m[:, par, SLOT[onto], s], op0=ALU.mult, op1=ALU.add)
                ins.then_inc(dve_scaled, 1)

            def add(q, c, step):
                par, b = c % 2, q * QBLOCKS + c
                rr = r[:, par, :, :]
                if step == 0:
                    dve.wait_ge(act_scaled, b * NA + 2 * NA)
                    dve.wait_ge(dve_scaled, b * ND + 2 * ND)
                    out, a, o = rr[:, 2, :], m[:, par, 4, :], m[:, par, 5, :]
                elif step == 1:
                    dve.wait_ge(pool_added, b * 2 + 6)
                    dve.wait_ge(chain, b * CHAIN + 2 * CHAIN + step)
                    out, a, o = rr[:, 2, :], rr[:, 2, :], rr[:, 0, :]
                else:
                    dve.wait_ge(chain, b * CHAIN + 2 * CHAIN + step)
                if step == 2:
                    out, a, o = rr[:, 2, 0:2 * S], rr[:, 2, 0:2 * S], rr[:, 2, 2 * S:4 * S]
                if step == 3:
                    dve.wait_ge(g_made, b + XD_AHEAD - 1)
                    out, a, o = y[:, par, :], rr[:, 2, 0:S], rr[:, 2, S:2 * S]
                nc.vector.tensor_tensor(out, a, o, ALU.add).then_inc(chain, 1)

            def scale_and_add(q, c, q_before, c_before):
                for j in range(ND):
                    scale(q, c, j)
                    add(q_before, c_before, j)

            def quad(q, more, products):
                scale_and_add(q, 2, q, 1)
                if more:
                    for step in range(CHAIN):
                        add(q, 2, step)
                    for tile in range(EARLY if products else 0):
                        product(q + 2, tile)
                    for j in range(ND):
                        scale(q, 3, j)
                        if j == 1:
                            split(q + 1, 0)
                        if products and EARLY + j < TILES:
                            product(q + 2, EARLY + j)
                    scale_and_add(q + 1, 0, q, 3)
                    scale_and_add(q + 1, 1, q + 1, 0)
                    split(q + 1, 1)
                else:
                    scale_and_add(q, 3, q, 2)
                    for step in range(CHAIN):
                        add(q, 3, step)

            for tile in range(TILES):
                product(0, tile)
            split(0, 0)
            split(0, 1)
            dve.wait_ge(consts_in, 96)
            for j in range(ND):
                scale(0, 0, j)
            for j in range(ND):
                scale(0, 1, j)
                add(0, 0, j)
                product(1, j)
            for tile in range(ND, TILES):
                product(1, tile)
            with dve.Fori(0, QUADS - 2) as q:
                quad(q, True, True)
            quad(QUADS - 2, True, False)
            quad(QUADS - 1, False, False)


def _pair_rows():
    direct = -np.ones((DT, F, TILES), np.int64)
    swapped = direct.copy()
    for k in range(DISTS):
        tile, kk = divmod(k, DT)
        for i in range(F):
            j = (i + k) % F
            direct[kk, i, tile] = i * F + j
            if k:
                swapped[kk, i, tile] = j * F + i
    return direct.reshape(ROWS, TILES), swapped.reshape(ROWS, TILES)


def kernel(**inputs):
    import concourse.bacc as _bacc
    from concourse.bass_utils import run_bass_kernel_spmd as _run

    def at(name):
        return np.asarray(inputs[name])

    tables = [at(f"tbl_{f}") for f in range(F)]
    starts = np.cumsum([0] + [tb.shape[0] for tb in tables[:-1]])
    assert starts[-1] + tables[-1].shape[0] < 1 << 24
    w0 = at("L0_rec_w0")
    w0x = np.concatenate([w0, np.zeros((1, S), w0.dtype)])
    direct, swapped = _pair_rows()
    ids = np.zeros((QUADS, PARTS * LOOKUPS, F), np.int32)
    ids[:, 0:QSAMPLES] = at("ids").reshape(QUADS, QSAMPLES, F)
    ids = ids.reshape(QUADS, PARTS, LOOKUPS, F).transpose(1, 3, 0, 2)
    arrays = {
        "tables": np.concatenate(tables),
        "ids": ids.reshape(LROWS, QUADS * LOOKUPS),
        "base": np.tile(starts, PARTS).astype(np.float32).reshape(LROWS, 1),
        "ident": np.eye(P, dtype=np.float32),
        "mask": np.repeat(np.eye(BLOCK_SAMPLES, dtype=np.float32), D, axis=0),
        "w0": w0x[direct],
        "w0t": w0x[swapped],
        "w1": at("L0_rec_w1"),
        "w2": at("L0_rec_w2"),
        "b0": at("L0_rec_b0").reshape(S, 1),
        "b1": at("L0_rec_b1").reshape(S),
        "b2": at("L0_rec_b2").reshape(S, 1),
        "dense": at("dense_ctx").T,
        "wt1": at("W_top1")[0:2 * S],
        "wt1d": at("W_top1")[2 * S:],
        "wt2": at("W_top2"),
        "wt3": at("W_top3").reshape(H2 // P, P).T,
        "bt1": at("b_top1").reshape(H1 // P, P).T,
        "bt2": at("b_top2").reshape(H2 // P, P).T,
    }
    arrays = {k: np.ascontiguousarray(a) for k, a in arrays.items()}
    nc = _bacc.Bacc("TRN2", target_bir_lowering=False, num_devices=1)
    t = {k: nc.dram_tensor(k + "_dram", a.shape, mybir.dt.from_np(a.dtype), kind="ExternalInput").ap()
         for k, a in arrays.items()}
    t["out"] = nc.dram_tensor("out_dram", (1, BATCH), F32, kind="ExternalOutput").ap()
    t["xt"] = nc.dram_tensor("xt_dram", (2 * F, POINTS), F32, kind="Internal").ap()
    bass_dlrm_cin_tower(nc, t)
    res = _run(nc, [{k + "_dram": a for k, a in arrays.items()}], core_ids=[0])
    return res.results[0]["out_dram"].reshape(BATCH, 1)
```

```python
from contextlib import ExitStack

import numpy as np

import concourse.bass as bass
from concourse import mybir

ALU = mybir.AluOpType
ACT = mybir.ActivationFunctionType
F32 = mybir.dt.float32
F32R = mybir.dt.float32r
I32 = mybir.dt.int32

P = 128
F = 39
D = 16
S = 128
BATCH = 1024
POINTS = BATCH * D
BLOCK_SAMPLES = P // D
QBLOCKS = 4
QPOINTS = QBLOCKS * P
QUADS = POINTS // QPOINTS
QSAMPLES = QBLOCKS * BLOCK_SAMPLES
SEGQ = 8
SEGMENTS = QUADS // SEGQ
SEGB = SEGQ * QSAMPLES
DISTS = F // 2 + 1
DT = 3
TILES = -(-DISTS // DT)
ROWS = DT * F
LAST_ROWS = (DISTS - (TILES - 1) * DT) * F
GROUPS = 10
GW = 4 * S
FX = F + 1
RING = 5
PARTS = P // F
LROWS = PARTS * F
LOOKUPS = -(-QSAMPLES // PARTS)
H1, H2 = 512, 256

ACT_GROUPS = (0, 2, 4, 5, 7, 9)
DVE_GROUPS = {1: 0, 3: 2, 6: 5, 8: 7}
SLOT = {0: 0, 4: 1, 2: 2, 5: 3, 7: 4, 9: 5}
NA, ND, SLOTS = len(ACT_GROUPS), len(DVE_GROUPS), len(SLOT)
STORED = 16 * 2 * PARTS
CHAIN = 4
LOOKS = (range(0), range(0, 2), range(2, 8), range(8, LOOKUPS))
SPLIT = (2, 3, 4, 5, 6)
SPLIT_FIRST, SPLIT_REST = SPLIT[0:1], SPLIT[1:]
NSPLIT = len(SPLIT)
POOL_TILE = TILES - 1
EARLY = 4
WARM_UP = 14
XD_AHEAD = QBLOCKS


def bass_dlrm_cin_tower(nc, t):
    with ExitStack() as ctx:
        def sb(name, shape, dt=F32):
            return ctx.enter_context(nc.sbuf_tensor(name, shape, dt))

        def psum(name, shape):
            return ctx.enter_context(nc.psum_tensor(name, shape, F32))

        def sem(name):
            return ctx.enter_context(nc.semaphore(name))

        ident = sb("ident", [P, P])
        mask = sb("mask", [P, BLOCK_SAMPLES])
        idx = sb("idx", [LROWS, QUADS * LOOKUPS], I32)
        idx_raw = sb("idx_raw", [LROWS, QUADS * LOOKUPS], I32)
        idx_now = sb("idx_now", [LROWS, LOOKUPS], I32)
        base = sb("base", [LROWS, 1])
        looked = sb("looked", [LROWS, LOOKUPS, D])
        looked1 = sb("looked1", [LROWS, LOOKUPS, D])
        fields = sb("fields", [ROWS, QPOINTS])
        pairs = sb("pairs", [P, TILES, QPOINTS])
        pairs_h = sb("pairs_h", [P, NSPLIT, QPOINTS], F32R)
        pairs_l = sb("pairs_l", [P, NSPLIT, QPOINTS], F32R)
        w0 = sb("w0", [ROWS, TILES, S])
        w0t = sb("w0t", [ROWS, TILES, S])
        w0h = sb("w0h", [ROWS, NSPLIT, S], F32R)
        w0l = sb("w0l", [ROWS, NSPLIT, S], F32R)
        w1h = sb("w1h", [P, F * S], F32R)
        w1l = sb("w1l", [P, F * S], F32R)
        w2 = sb("w2", [P, F, S])
        b0 = sb("b0", [P, 1])
        b2 = sb("b2", [P, 1])
        b2x = sb("b2x", [P, 1])
        x = sb("x", [P, QBLOCKS, FX])
        vh = sb("vh", [P, QPOINTS], F32R)
        vl = sb("vl", [P, QPOINTS], F32R)
        m = sb("m", [P, 2, SLOTS, GW])
        r = sb("r", [P, 2, SLOTS // 2, GW])
        y = sb("y", [P, 2, S])
        xd = sb("xd", [P, XD_AHEAD, FX, BLOCK_SAMPLES])
        g = sb("g", [P, FX, SEGB])
        z1 = sb("z1", [P, BATCH])
        z2 = sb("z2", [P, BATCH])
        bt1 = sb("bt1", [P, H1 // P])
        bt2 = sb("bt2", [P, H2 // P])
        wt3 = sb("wt3", [P, H2 // P])
        w1raw = g[:].rearrange("p i b -> p (i b)")[:, 0:F * S]
        idx_f = r[0:LROWS, 0, 0, 0:QUADS * LOOKUPS]
        wt1 = pairs[:, 0:2, :]
        wt2 = pairs[:, 2:4, :].rearrange("p a (c n) -> p (a c) n", n=H2)
        wt1d = pairs[0:D, 4, :]
        dense = pairs[0:D, 5:7, :]
        hidden = m[:].rearrange("p a c n -> p (a c) n")
        h1 = hidden[:, 0:8, :].rearrange("p (a f) n -> p a f n", a=2)
        h2 = hidden[:, 8:12, :].rearrange("p (a f) n -> p a f n", a=2)
        out_row = r[0:1, 0, 0:2, :]

        pt = psum("pt", [P, RING, GW])
        pv = psum("pv", [P, QPOINTS])
        pg = psum("pg", [P, GW])
        px = psum("px", [P, GW])
        pxt = px[:, 0:QBLOCKS * F].rearrange("p (c i) -> p c i", i=F)
        pz = px[:, SEGB:2 * SEGB]

        idx_in = sem("idx_in")
        consts_in = sem("consts_in")
        w0_in = sem("w0_in")
        w1_in = sem("w1_in")
        w2_in = sem("w2_in")
        mlp_in = sem("mlp_in")
        prep = sem("prep")
        idx_ready = sem("idx_ready")
        w0_ready = sem("w0_ready")
        w0h_ready = sem("w0h_ready")
        w0l_ready = sem("w0l_ready")
        w1h_ready = sem("w1h_ready")
        w1l_ready = sem("w1l_ready")
        b2_ready = sem("b2_ready")
        idx_staged = sem("idx_staged")
        looked_up = sem("looked_up")
        looked1_up = sem("looked1_up")
        xt_stored = sem("xt_stored")
        fields_in = sem("fields_in")
        pairs_in = [sem(f"pairs_in{i}") for i in range(TILES)]
        pairs_ready = sem("pairs_ready")
        pool_pairs_ready = sem("pool_pairs_ready")
        pairs_rounded = sem("pairs_rounded")
        pairs_split = sem("pairs_split")
        pairs_used = sem("pairs_used")
        xt_turned = sem("xt_turned")
        x_one = sem("x_one")
        x_ready = sem("x_ready")
        vh_ready = sem("vh_ready")
        vl_ready = sem("vl_ready")
        t_ready = sem("t_ready")
        act_scaled = sem("act_scaled")
        dve_scaled = sem("dve_scaled")
        pool_added = sem("pool_added")
        chain = sem("chain")
        xd_ready = sem("xd_ready")
        g_made = sem("g_made")
        g_kept = sem("g_kept")
        l2_done = sem("l2_done")
        z_kept = sem("z_kept")
        z1_kept = sem("z1_kept")
        h_made = sem("h_made")
        h_kept = sem("h_kept")
        out_done = sem("out_done")

        xt_dram = t["xt"]

        block = ctx.enter_context(nc.Block())

        @block.sync
        def _(sp):
            sp.dma_start(idx_raw[:], t["ids"]).then_inc(idx_in, 16)
            sp.dma_start(base[:], t["base"]).then_inc(idx_in, 16)
            sp.dma_start(w0[:], t["w0"]).then_inc(w0_in, 16)
            sp.dma_start(w0t[:], t["w0t"]).then_inc(w0_in, 16)
            sp.dma_start(ident[:], t["ident"]).then_inc(consts_in, 16)
            sp.dma_start(mask[:], t["mask"]).then_inc(consts_in, 16)
            sp.dma_start(b0[:], t["b0"]).then_inc(consts_in, 16)
            sp.dma_start(b2[:], t["b2"]).then_inc(consts_in, 16)
            sp.dma_start(w1raw.rearrange("p (i s) -> p i s", s=S), t["w1"].rearrange("(i j) s -> j i s", j=S)).then_inc(w1_in, 16)
            for half in range(2):
                sp.dma_start(m[:, half, SLOT[GROUPS - 1], 3 * S:4 * S], t["b1"].partition_broadcast(P)).then_inc(consts_in, 16)

            def store(q, looked, landed, before):
                sp.wait_ge(landed, (before + 1) * (16 * LOOKUPS))
                for part in range(PARTS):
                    n = min(LOOKUPS, QSAMPLES - part * LOOKUPS)
                    src = looked[part * F:(part + 1) * F, 0:n, :].rearrange("f c d -> f (c d)")
                    for copy in range(2):
                        dst = xt_dram[copy * F:(copy + 1) * F, bass.ds(q * QPOINTS + part * (LOOKUPS * D), n * D)]
                        sp.dma_start(dst, src).then_inc(xt_stored, 16)

            def rows_of(q, first, step, n):
                return bass.AP(tensor=xt_dram.tensor, offset=q * QPOINTS + first * POINTS,
                               ap=[[step * POINTS, n], [POINTS, F], [1, QPOINTS]])

            def load(q):
                sp.wait_ge(xt_stored, (q + 1) * STORED)
                sp.wait_ge(pairs_ready, q * POOL_TILE + 1)
                sp.wait_ge(pool_pairs_ready, q + 1)
                sp.wait_ge(xt_turned, q + 1)
                sp.dma_start(fields[:], rows_of(q, 0, 0, DT)).then_inc(fields_in, 16)
                for tile in range(TILES):
                    sp.wait_ge(pairs_used, q * TILES + tile + 1)
                    n = DT if tile < TILES - 1 else LAST_ROWS // F
                    sp.dma_start(pairs[0:n * F, tile, :], rows_of(q, tile * DT, 1, n)).then_inc(pairs_in[tile], 16)

            store(0, looked, looked_up, 0)
            load(0)
            store(1, looked1, looked1_up, 0)
            load(1)
            store(2, looked, looked_up, 1)
            load(2)
            sp.dma_start(w2[:], t["w2"].rearrange("(i j) s -> j i s", j=S)).then_inc(w2_in, 16)
            sp.dma_start(bt1[:], t["bt1"]).then_inc(mlp_in, 16)
            sp.dma_start(bt2[:], t["bt2"]).then_inc(mlp_in, 16)
            sp.dma_start(wt3[:], t["wt3"]).then_inc(mlp_in, 16)
            with sp.Fori(3, QUADS) as q:
                store(q, looked, looked_up, q - 1)
                load(q)
            sp.wait_ge(pairs_used, (QUADS + 1) * TILES)
            sp.dma_start(wt1, t["wt1"].rearrange("(c p) n -> p c n", p=P)).then_inc(mlp_in, 16)
            sp.dma_start(wt1d, t["wt1d"]).then_inc(mlp_in, 16)
            sp.dma_start(dense.rearrange("p a n -> p (a n)"), t["dense"]).then_inc(mlp_in, 16)
            sp.dma_start(wt2, t["wt2"].rearrange("(c p) n -> p c n", p=P)).then_inc(mlp_in, 16)
            sp.wait_ge(h_kept, 2 * (H1 + H2) // P + 2)
            sp.dma_start(t["out"], out_row.rearrange("p a n -> p (a n)")).then_inc(out_done, 16)
            sp.wait_ge(out_done, 16)

        @block.gpsimd
        def _(pool):
            pool.sem_inc(pool_added, 4)
            pool.sem_inc(pool_pairs_ready, 1)
            pool.wait_ge(idx_ready, 1)

            def stage(q):
                pool.wait_ge(xt_stored, q * STORED)
                nc.gpsimd.tensor_copy(idx_now[:], idx[:, bass.ds(q * LOOKUPS, LOOKUPS)]).then_inc(idx_staged, 1)

            def lookups(which, rows=idx_now, looked=looked, landed=looked_up):
                for n in which:
                    nc.gpsimd.indirect_dma_start(
                        out=looked[:, n, :], out_offset=None, in_=t["tables"],
                        in_offset=bass.IndirectOffsetOnAxis(ap=rows[:, n:n + 1], axis=0),
                    ).then_inc(landed, 16)

            def diagonal(q, c):
                b = q * QBLOCKS + c
                pool.wait_ge(x_ready, q * 2 + (3 if c < 3 else 4))
                pool.wait_ge(g_made, b + 1)
                nc.gpsimd.tensor_tensor(
                    xd[:, c, :, :], x[:, c, :].unsqueeze(2).to_broadcast([P, FX, BLOCK_SAMPLES]),
                    mask[:].unsqueeze(1).to_broadcast([P, FX, BLOCK_SAMPLES]), ALU.mult).then_inc(xd_ready, 1)

            def add(q, c):
                par, b = c % 2, q * QBLOCKS + c
                pool.wait_ge(act_scaled, b * NA + NA + 4)
                pool.wait_ge(dve_scaled, b * ND + ND + 3)
                pool.wait_ge(chain, b * CHAIN + 2)
                nc.gpsimd.tensor_tensor(r[:, par, 0:2, :], m[:, par, 0:2, :], m[:, par, 2:4, :], ALU.add).then_inc(pool_added, 1)
                pool.wait_ge(pool_added, b * 2 + 5)
                nc.gpsimd.tensor_tensor(r[:, par, 0, :], r[:, par, 0, :], r[:, par, 1, :], ALU.add).then_inc(pool_added, 1)

            def product(q):
                rows = LAST_ROWS
                pool.wait_ge(fields_in, (q + 1) * 16)
                pool.wait_ge(pairs_in[POOL_TILE], (q + 1) * 16)
                nc.gpsimd.tensor_tensor(pairs[0:rows, POOL_TILE, :], pairs[0:rows, POOL_TILE, :], fields[0:rows, :],
                                        ALU.mult).then_inc(pool_pairs_ready, 1)

            lookups(range(LOOKUPS), idx[:, 0:LOOKUPS])
            lookups(range(LOOKUPS), idx[:, LOOKUPS:2 * LOOKUPS], looked1, looked1_up)
            product(0)
            pool.wait_ge(xt_stored, STORED)
            lookups(range(LOOKUPS), idx[:, 2 * LOOKUPS:3 * LOOKUPS])
            pool.wait_ge(consts_in, 96)
            pool.wait_ge(x_one, 1)

            def quad(q, look, more=True):
                for c in range(QBLOCKS):
                    diagonal(q, c)
                    if look and c == 1:
                        pool.wait_ge(idx_staged, q + 1)
                    add(q, c)
                    if more and c == 0:
                        product(q + 1)
                    if look and c == 0:
                        stage(q + 3)
                    if look:
                        lookups(LOOKS[c])

            with pool.Fori(0, QUADS - 3) as q:
                quad(q, True)
            with pool.Fori(QUADS - 3, QUADS - 1) as q:
                quad(q, False)
            quad(QUADS - 1, False, more=False)

        @block.tensor
        def _(pe):
            pe.sem_inc(g_made, XD_AHEAD)
            pe.sem_inc(pairs_used, TILES)
            pe.sem_inc(xt_turned, 1)

            def layer0(q, split, between=None):
                pe.wait_ge(fields_in, (q + 1) * 16)
                pe.wait_ge(x_ready, q * 2 + 2)
                for c in range(QBLOCKS):
                    n = ROWS if c == 0 else F
                    mm = pe.transpose(px[:, c * F:c * F + n], fields[0:n, c * P:(c + 1) * P], ident[0:n, 0:n])
                mm.then_inc(xt_turned, 1)
                pe.wait_ge(vl_ready, q * 2 + 2)
                for tile in range(TILES):
                    if tile == 3 and between:
                        between()
                    rows = ROWS if tile < TILES - 1 else LAST_ROWS
                    whole = pairs[0:rows, tile, :]
                    start, stop = tile == 0, tile == TILES - 1
                    if split and tile in SPLIT:
                        j = SPLIT.index(tile)
                        pe.wait_ge(pairs_split, (q - 1) * NSPLIT + j + 1)
                        pe.matmul(pv[:, :], w0h[0:rows, j, :], pairs_h[0:rows, j, :], start=start, stop=False)
                        pe.matmul(pv[:, :], w0l[0:rows, j, :], pairs_h[0:rows, j, :], start=False, stop=False)
                        mm = pe.matmul(pv[:, :], w0h[0:rows, j, :], pairs_l[0:rows, j, :], start=False, stop=stop)
                    else:
                        if tile == POOL_TILE:
                            pe.wait_ge(pool_pairs_ready, q + 2)
                        else:
                            pe.wait_ge(pairs_ready, q * POOL_TILE + tile + 2)
                        mm = pe.matmul(pv[:, :], w0[0:rows, tile, :], whole, start=start, stop=stop)
                    mm.then_inc(pairs_used, 1)

            def layer1(q, c, between=None):
                b = q * QBLOCKS + c
                pe.wait_ge(vh_ready, q * 2 + (3 if c < 3 else 4))
                pe.wait_ge(vl_ready, q * 2 + (3 if c < 3 else 4))
                pts = slice(c * P, (c + 1) * P)
                for n in range(GROUPS):
                    if n == RING and between:
                        between()
                    last = (n + RING) % GROUPS
                    before = b if n >= RING else b - 1
                    if last in ACT_GROUPS:
                        pe.wait_ge(act_scaled, before * NA + NA + ACT_GROUPS.index(last) + 1)
                    else:
                        pe.wait_ge(dve_scaled, before * ND + ND + list(DVE_GROUPS).index(last) + 1)
                    cols = slice(n * GW, min((n + 1) * GW, F * S))
                    w = cols.stop - cols.start
                    out = pt[:, n % RING, 0:w]
                    pe.matmul(out, vh[:, pts], w1h[:, cols], start=True, stop=False)
                    pe.matmul(out, vh[:, pts], w1l[:, cols], start=False, stop=False)
                    pe.matmul(out, vl[:, pts], w1h[:, cols], start=False, stop=True).then_inc(t_ready, 1)

            def gram(q, c):
                par, b = c % 2, q * QBLOCKS + c
                pe.wait_ge(chain, b * CHAIN + 3 * CHAIN)
                pe.wait_ge(xd_ready, b + 1)
                pe.wait_ge(g_kept, b + 1)
                pe.matmul(pg[:, 0:FX * BLOCK_SAMPLES], y[:, par, :],
                          xd[:, c, :, :].rearrange("p i b -> p (i b)"), start=True, stop=True).then_inc(g_made, 1)

            def layer2(seg, more):
                pe.wait_ge(w2_in, 16)
                pe.wait_ge(g_kept, (seg + 1) * (SEGQ * QBLOCKS) + 1)
                pe.wait_ge(z_kept, seg + 1)
                if more:
                    pe.wait_ge(x_ready, (seg + 1) * (SEGQ * 2) + 4)
                for i in range(F):
                    mm = pe.matmul(pz, w2[:, i, :], g[:, i, :], start=(i == 0), stop=(i == F - 1))
                mm.then_inc(l2_done, 1)

            def hidden1(half):
                cols = slice(half * 512, (half + 1) * 512)
                for f in range(H1 // P):
                    out = pt[:, f, :]
                    fs = slice(f * P, (f + 1) * P)
                    if half:
                        pe.wait_ge(h_kept, f + 1)
                    pe.matmul(out, wt1[:, 0, fs], z1[:, cols], start=True, stop=False)
                    pe.matmul(out, wt1[:, 1, fs], z2[:, cols], start=False, stop=False)
                    pe.matmul(out, wt1d[:, fs], dense[:, half, :], start=False, stop=True).then_inc(h_made, 1)

            def quad(q, more):
                layer1(q, 2, lambda: gram(q, 0))
                if more:
                    layer0(q + 1, True, lambda: gram(q, 1))
                    layer1(q, 3, lambda: gram(q, 2))
                    layer1(q + 1, 0)
                    layer1(q + 1, 1, lambda: gram(q, 3))
                else:
                    layer1(q, 3, lambda: gram(q, 1))
                    gram(q, 2)
                    pe.wait_ge(mlp_in, 7 * 16)
                    pe.wait_ge(z_kept, SEGMENTS)
                    pe.wait_ge(z1_kept, SEGMENTS - 1)
                    pe.wait_ge(act_scaled, (QUADS * QBLOCKS + 1) * NA)
                    pe.wait_ge(dve_scaled, (QUADS * QBLOCKS + 1) * ND)
                    hidden1(0)
                    gram(q, 3)

            pe.wait_ge(consts_in, 96)
            pe.wait_ge(w0_ready, 1)
            pe.wait_ge(looked_up, 16 * LOOKUPS)
            for _ in range(WARM_UP):
                pe.matmul(px[:, 0:P], ident[:], ident[:], start=True, stop=True)
            layer0(0, False)
            pe.wait_ge(w1h_ready, 1)
            pe.wait_ge(w1l_ready, 1)
            layer1(0, 0)
            layer1(0, 1)
            pe.wait_ge(w0l_ready, 1)
            with pe.Fori(0, SEGMENTS - 1) as seg:
                with pe.Fori(0, SEGQ) as k:
                    quad(seg * SEGQ + k, True)
                layer2(seg, True)
            with pe.Fori(QUADS - SEGQ, QUADS - 1) as q:
                quad(q, True)
            quad(QUADS - 1, False)
            layer2(SEGMENTS - 1, False)

            pe.wait_ge(z_kept, SEGMENTS + 1)
            pe.wait_ge(z1_kept, SEGMENTS)
            hidden1(1)
            kept = 2 * H1 // P
            for half in range(2):
                for f in range(H2 // P):
                    pe.wait_ge(h_kept, kept)
                    out = pt[:, 2 * half + f, :]
                    for c in range(H1 // P):
                        mm = pe.matmul(out, wt2[:, c, f * P:(f + 1) * P], h1[:, half, c, :],
                                       start=(c == 0), stop=(c == H1 // P - 1))
                    mm.then_inc(h_made, 1)
            kept += 2 * H2 // P
            for half in range(2):
                pe.wait_ge(h_kept, kept)
                out = (pv if half else pg)[0:1, :]
                for c in range(H2 // P):
                    mm = pe.matmul(out, wt3[:, c:c + 1], h2[:, half, c, :], start=(c == 0), stop=(c == H2 // P - 1))
                mm.then_inc(h_made, 1)

        @block.scalar
        def _(act):
            act.sem_inc(act_scaled, NA)
            act.sem_inc(g_kept, 1)
            act.sem_inc(z_kept, 1)
            act.sem_inc(x_ready, 2)
            act.sem_inc(vh_ready, 2)

            act.wait_ge(consts_in, 96)
            nc.scalar.activation(b2x[:], b2[:], ACT.Copy, scale=float(D)).then_inc(b2_ready, 1)
            act.wait_ge(w1_in, 16)
            nc.scalar.activation(w1h[:], w1raw, ACT.Copy).then_inc(w1h_ready, 1)
            act.wait_ge(w0_ready, 1)
            nc.scalar.activation(w0h[:], w0[:, SPLIT[0]:SPLIT[0] + NSPLIT, :], ACT.Copy).then_inc(w0h_ready, 1)

            def keep_x(q, part, first=False):
                blocks = slice(0, 3) if part == 0 else slice(3, 4)
                before = q * QBLOCKS - 1 + part
                act.wait_ge(xt_turned, q + 2)
                if not first:
                    act.wait_ge(dve_scaled, before * ND + ND)
                    act.wait_ge(xd_ready, before)
                    act.wait_ge(act_scaled, before * NA + NA)
                nc.scalar.activation(x[:, blocks, 0:F], pxt[:, blocks, :], ACT.Copy).then_inc(x_ready, 1)

            def keep_v(q, part, first=False):
                pts = slice(0, 3 * P) if part == 0 else slice(3 * P, 4 * P)
                before = q * QBLOCKS - 1 + part
                act.wait_ge(pairs_used, (q + 2) * TILES)
                if not first:
                    act.wait_ge(t_ready, before * GROUPS)
                act.wait_ge(vl_ready, q * 2 + part + 2)
                nc.scalar.activation(vh[:, pts], pv[:, pts], ACT.Identity, bias=b0[:, 0:1]).then_inc(vh_ready, 1)

            def round_pairs(q, tiles):
                for tile in tiles:
                    rows = ROWS if tile < TILES - 1 else LAST_ROWS
                    if tile == POOL_TILE:
                        act.wait_ge(pool_pairs_ready, q + 2)
                    else:
                        act.wait_ge(pairs_ready, q * POOL_TILE + tile + 2)
                    nc.scalar.activation(pairs_h[0:rows, SPLIT.index(tile), :], pairs[0:rows, tile, :],
                                         ACT.Copy).then_inc(pairs_rounded, 1)

            def scale(q, c, groups=ACT_GROUPS):
                par, b = c % 2, q * QBLOCKS + c
                if 0 in groups:
                    act.wait_ge(x_ready, q * 2 + (3 if c < 3 else 4))
                    act.wait_ge(pool_added, b * 2 + 1)
                    act.wait_ge(chain, b * CHAIN + 1)
                for n in groups:
                    act.wait_ge(t_ready, b * GROUPS + n + 1)
                    fs = range(4 * n, min(4 * n + 4, F))
                    for i in fs:
                        s = slice((i % 4) * S, (i % 4 + 1) * S)
                        ins = nc.scalar.activation(m[:, par, SLOT[n], s], pt[:, n % RING, s], ACT.Copy, scale=x[:, c, i:i + 1])
                    ins.then_inc(act_scaled, 1)

            def keep_g(q, c, k):
                b = q * QBLOCKS + c
                act.wait_ge(g_made, b + XD_AHEAD + 1)
                nc.scalar.activation(g[:, :, bass.ds(k * QSAMPLES + c * BLOCK_SAMPLES, BLOCK_SAMPLES)],
                                     pg[:, 0:FX * BLOCK_SAMPLES].rearrange("p (i b) -> p i b", i=FX),
                                     ACT.Copy).then_inc(g_kept, 1)

            made = [0]

            def keep_hidden(hid, bias, bank, half):
                for f in range(hid.shape[2]):
                    made[0] += 1
                    act.wait_ge(h_made, made[0])
                    nc.scalar.activation(hid[:, half, f, :], pt[:, bank + f, :], ACT.Relu, bias=bias[:, f:f + 1]).then_inc(h_kept, 1)

            def quad(q, k, more, ahead=True):
                scale(q, 2)
                keep_g(q, 0, k)
                if more:
                    round_pairs(q + 1, SPLIT_REST)
                    keep_g(q, 1, k)
                    scale(q, 3, ACT_GROUPS[0:2])
                    keep_x(q + 1, 0)
                    keep_v(q + 1, 0)
                    scale(q, 3, ACT_GROUPS[2:])
                    keep_g(q, 2, k)
                    scale(q + 1, 0)
                    keep_x(q + 1, 1)
                    scale(q + 1, 1, ACT_GROUPS[0:2])
                    if ahead:
                        round_pairs(q + 2, SPLIT_FIRST)
                    scale(q + 1, 1, ACT_GROUPS[2:])
                    keep_g(q, 3, k)
                    keep_v(q + 1, 1)
                else:
                    scale(q, 3)
                    keep_g(q, 1, k)
                    keep_g(q, 2, k)
                    act.wait_ge(mlp_in, 7 * 16)
                    act.wait_ge(pool_added, QUADS * QBLOCKS * 2 + 2)
                    act.wait_ge(chain, (QUADS * QBLOCKS + 1) * CHAIN)
                    keep_hidden(h1, bt1, 0, 0)
                    keep_g(q, 3, k)

            def keep_z(seg):
                act.wait_ge(g_kept, (seg + 1) * (SEGQ * QBLOCKS) + 1)
                nc.scalar.activation(z1[:, bass.ds(seg * SEGB, SEGB)], g[:, F, :], ACT.Copy).then_inc(z1_kept, 1)
                act.wait_ge(l2_done, seg + 1)
                nc.scalar.activation(z2[:, bass.ds(seg * SEGB, SEGB)], pz, ACT.Identity, bias=b2x[:, 0:1]).then_inc(z_kept, 1)

            act.wait_ge(x_one, 1)
            for part in range(2):
                keep_x(0, part, first=True)
                keep_v(0, part, first=True)
            act.wait_ge(b2_ready, 1)
            scale(0, 0)
            scale(0, 1, ACT_GROUPS[0:2])
            round_pairs(1, SPLIT_FIRST)
            scale(0, 1, ACT_GROUPS[2:])
            with act.Fori(0, SEGMENTS - 1) as seg:
                with act.Fori(0, SEGQ) as k:
                    quad(seg * SEGQ + k, k, True)
                keep_z(seg)
            with act.Fori(QUADS - SEGQ, QUADS - 2) as q:
                quad(q, q - (QUADS - SEGQ), True)
            quad(QUADS - 2, SEGQ - 2, True, ahead=False)
            quad(QUADS - 1, SEGQ - 1, False)
            keep_z(SEGMENTS - 1)

            keep_hidden(h1, bt1, 0, 1)
            for half in range(2):
                keep_hidden(h2, bt2, 2 * half, half)
            for half in range(2):
                act.wait_ge(h_made, 2 * (H1 + H2) // P + 1 + half)
                nc.scalar.activation(out_row[:, half, :], (pv if half else pg)[0:1, :], ACT.Copy).then_inc(h_kept, 1)

        @block.vector
        def _(dve):
            dve.sem_inc(dve_scaled, ND)
            dve.sem_inc(chain, 2 * CHAIN)
            dve.sem_inc(pairs_ready, 1)
            dve.sem_inc(vl_ready, 2)
            nc.vector.memset(x[:, :, F:FX], 1.0).then_inc(x_one, 1)

            dve.wait_ge(idx_in, 32)
            nc.vector.tensor_copy(idx_f, idx_raw[:]).then_inc(prep, 1)
            dve.wait_ge(prep, 1)
            nc.vector.tensor_scalar(idx[:], idx_f, base[:, 0:1], None, ALU.add).then_inc(idx_ready, 1)
            dve.wait_ge(w0_in, 32)
            nc.vector.tensor_tensor(w0[:], w0[:], w0t[:], ALU.add).then_inc(w0_ready, 1)
            dve.wait_ge(w1h_ready, 1)
            nc.vector.tensor_tensor(w1l[:], w1raw, w1h[:].bitcast(F32), ALU.subtract).then_inc(w1l_ready, 1)

            dve.wait_ge(w0h_ready, 1)
            nc.vector.tensor_tensor(w0l[:], w0[:, SPLIT[0]:SPLIT[0] + NSPLIT, :], w0h[:].bitcast(F32), ALU.subtract).then_inc(w0l_ready, 1)

            def product(q, tile):
                dve.wait_ge(fields_in, (q + 1) * 16)
                dve.wait_ge(pairs_in[tile], (q + 1) * 16)
                nc.vector.tensor_tensor(pairs[0:ROWS, tile, :], pairs[0:ROWS, tile, :], fields[:],
                                        ALU.mult).then_inc(pairs_ready, 1)

            def split_pairs(q, tiles):
                for tile in tiles:
                    rows = ROWS if tile < TILES - 1 else LAST_ROWS
                    j = SPLIT.index(tile)
                    dve.wait_ge(pairs_rounded, (q - 1) * NSPLIT + j + 1)
                    nc.vector.tensor_tensor(pairs_l[0:rows, j, :], pairs[0:rows, tile, :], pairs_h[0:rows, j, :].bitcast(F32),
                                            ALU.subtract).then_inc(pairs_split, 1)

            def split_v(q, part):
                pts = slice(0, 3 * P) if part == 0 else slice(3 * P, 4 * P)
                dve.wait_ge(vh_ready, q * 2 + part + 3)
                nc.vector.scalar_tensor_tensor(out=vl[:, pts], in0=pv[:, pts], scalar=b0[:, 0:1], in1=vh[:, pts].bitcast(F32),
                                               op0=ALU.add, op1=ALU.subtract).then_inc(vl_ready, 1)

            def scale(q, c, j):
                par, b = c % 2, q * QBLOCKS + c
                n, onto = list(DVE_GROUPS.items())[j]
                if j == 0:
                    dve.wait_ge(x_ready, q * 2 + (3 if c < 3 else 4))
                dve.wait_ge(act_scaled, b * NA + NA + ACT_GROUPS.index(onto) + 1)
                dve.wait_ge(t_ready, b * GROUPS + n + 1)
                for i in range(4):
                    s = slice(i * S, (i + 1) * S)
                    ins = nc.vector.scalar_tensor_tensor(
                        out=m[:, par, SLOT[onto], s], in0=pt[:, n % RING, s], scalar=x[:, c, 4 * n + i:4 * n + i + 1],
                        in1=m[:, par, SLOT[onto], s], op0=ALU.mult, op1=ALU.add)
                ins.then_inc(dve_scaled, 1)

            def add(q, c, step):
                par, b = c % 2, q * QBLOCKS + c
                rr = r[:, par, :, :]
                if step == 0:
                    dve.wait_ge(act_scaled, b * NA + 2 * NA)
                    dve.wait_ge(dve_scaled, b * ND + 2 * ND)
                    out, a, o = rr[:, 2, :], m[:, par, 4, :], m[:, par, 5, :]
                elif step == 1:
                    dve.wait_ge(pool_added, b * 2 + 6)
                    dve.wait_ge(chain, b * CHAIN + 2 * CHAIN + step)
                    out, a, o = rr[:, 2, :], rr[:, 2, :], rr[:, 0, :]
                else:
                    dve.wait_ge(chain, b * CHAIN + 2 * CHAIN + step)
                if step == 2:
                    out, a, o = rr[:, 2, 0:2 * S], rr[:, 2, 0:2 * S], rr[:, 2, 2 * S:4 * S]
                if step == 3:
                    dve.wait_ge(g_made, b + XD_AHEAD - 1)
                    out, a, o = y[:, par, :], rr[:, 2, 0:S], rr[:, 2, S:2 * S]
                nc.vector.tensor_tensor(out, a, o, ALU.add).then_inc(chain, 1)

            def scale_and_add(q, c, q_before, c_before):
                for j in range(ND):
                    scale(q, c, j)
                    add(q_before, c_before, j)

            def quad(q, more, products):
                scale_and_add(q, 2, q, 1)
                if more:
                    split_pairs(q + 1, SPLIT_REST)
                    for step in range(max(CHAIN, EARLY)):
                        if step < CHAIN:
                            add(q, 2, step)
                        if step < EARLY and products:
                            product(q + 2, step)
                    for j in range(ND):
                        scale(q, 3, j)
                        if j == 1:
                            split_v(q + 1, 0)
                    if products:
                        product(q + 2, EARLY)
                    scale_and_add(q + 1, 0, q, 3)
                    if products and EARLY + 1 < POOL_TILE:
                        product(q + 2, EARLY + 1)
                    scale_and_add(q + 1, 1, q + 1, 0)
                    if products:
                        split_pairs(q + 2, SPLIT_FIRST)
                    split_v(q + 1, 1)
                else:
                    scale_and_add(q, 3, q, 2)
                    for step in range(CHAIN):
                        add(q, 3, step)

            for tile in range(POOL_TILE):
                product(0, tile)
            split_v(0, 0)
            split_v(0, 1)
            dve.wait_ge(consts_in, 96)
            for j in range(ND):
                scale(0, 0, j)
                product(1, j)
            for j in range(ND):
                scale(0, 1, j)
                add(0, 0, j)
                if ND + j < POOL_TILE:
                    product(1, ND + j)
            split_pairs(1, SPLIT_FIRST)
            with dve.Fori(0, QUADS - 2) as q:
                quad(q, True, True)
            quad(QUADS - 2, True, False)
            quad(QUADS - 1, False, False)


def _pair_rows():
    direct = -np.ones((DT, F, TILES), np.int64)
    swapped = direct.copy()
    for k in range(DISTS):
        tile, kk = divmod(k, DT)
        for i in range(F):
            j = (i + k) % F
            direct[kk, i, tile] = i * F + j
            if k:
                swapped[kk, i, tile] = j * F + i
    return direct.reshape(ROWS, TILES), swapped.reshape(ROWS, TILES)


def kernel(**inputs):
    import concourse.bacc as _bacc
    from concourse.bass_utils import run_bass_kernel_spmd as _run

    def at(name):
        return np.asarray(inputs[name])

    tables = [at(f"tbl_{f}") for f in range(F)]
    starts = np.cumsum([0] + [tb.shape[0] for tb in tables[:-1]])
    assert starts[-1] + tables[-1].shape[0] < 1 << 24
    w0 = at("L0_rec_w0")
    w0x = np.concatenate([w0, np.zeros((1, S), w0.dtype)])
    direct, swapped = _pair_rows()
    ids = np.zeros((QUADS, PARTS * LOOKUPS, F), np.int32)
    ids[:, 0:QSAMPLES] = at("ids").reshape(QUADS, QSAMPLES, F)
    ids = ids.reshape(QUADS, PARTS, LOOKUPS, F).transpose(1, 3, 0, 2)
    arrays = {
        "tables": np.concatenate(tables),
        "ids": ids.reshape(LROWS, QUADS * LOOKUPS),
        "base": np.tile(starts, PARTS).astype(np.float32).reshape(LROWS, 1),
        "ident": np.eye(P, dtype=np.float32),
        "mask": np.repeat(np.eye(BLOCK_SAMPLES, dtype=np.float32), D, axis=0),
        "w0": w0x[direct],
        "w0t": w0x[swapped],
        "w1": at("L0_rec_w1"),
        "w2": at("L0_rec_w2"),
        "b0": at("L0_rec_b0").reshape(S, 1),
        "b1": at("L0_rec_b1").reshape(S),
        "b2": at("L0_rec_b2").reshape(S, 1),
        "dense": at("dense_ctx").T,
        "wt1": at("W_top1")[0:2 * S],
        "wt1d": at("W_top1")[2 * S:],
        "wt2": at("W_top2"),
        "wt3": at("W_top3").reshape(H2 // P, P).T,
        "bt1": at("b_top1").reshape(H1 // P, P).T,
        "bt2": at("b_top2").reshape(H2 // P, P).T,
    }
    arrays = {k: np.ascontiguousarray(a) for k, a in arrays.items()}
    nc = _bacc.Bacc("TRN2", target_bir_lowering=False, num_devices=1)
    t = {k: nc.dram_tensor(k + "_dram", a.shape, mybir.dt.from_np(a.dtype), kind="ExternalInput").ap()
         for k, a in arrays.items()}
    t["out"] = nc.dram_tensor("out_dram", (1, BATCH), F32, kind="ExternalOutput").ap()
    t["xt"] = nc.dram_tensor("xt_dram", (2 * F, POINTS), F32, kind="Internal").ap()
    bass_dlrm_cin_tower(nc, t)
    res = _run(nc, [{k + "_dram": a for k, a in arrays.items()}], core_ids=[0])
    return res.results[0]["out_dram"].reshape(BATCH, 1)
```
